# Optimizing a Trainium2 kernel written in Bass

```python
import numpy as np
import jax
import jax.numpy as jnp

def _softmax(x, axis=-1):
    return jax.nn.softmax(x, axis=axis)

def _gelu(x):
    return jax.nn.gelu(x, approximate=True)

def _silu(x):
    return jax.nn.silu(x)

def _sigmoid(x):
    return jax.nn.sigmoid(x)

def _layernorm(x, axis=-1, eps=1e-05):
    m = jnp.mean(x, axis=axis, keepdims=True)
    v = jnp.var(x, axis=axis, keepdims=True)
    return (x - m) / jnp.sqrt(v + eps)

def _scatter_add(tgt, idx, src, axis=0):
    return tgt.at[idx].add(src)

def _segment_sum(src, seg, n):
    return jax.ops.segment_sum(src, seg, n)
kernel_name = 'mk_adj_resnorm_d2_adj_r2_fbef66'

def setup_inputs(seed: int=0):
    np.random.seed(seed)
    _w = jnp.asarray

    def _rec_inputs():
        import jax
        import jax.numpy as jnp
        _gk = jax.random.key(seed)
        x = -0.0003929 + 0.9999 * jax.random.normal(jax.random.fold_in(_gk, 1), (32, 256, 256), jnp.float32)
        _a = jax.random.bernoulli(jax.random.fold_in(_gk, 2), 0.0078125, (256, 256))
        _a = jnp.logical_or(_a, jnp.eye(256, dtype=bool))
        _af = _a.astype(jnp.float32)
        _af = _af * jax.random.uniform(jax.random.fold_in(_gk, 3), (256, 256), jnp.float32, 0.05, 1)
        adj = _af
        return (x, adj)
    x, adj = _rec_inputs()

    def _L0_gnn_setup():
        import jax, jax.numpy as jnp
        import numpy as np
        B, N, D, O = (8, 2048, 256, 256)
        key = jax.random.key(seed)
        k1, k2, k3, k4 = jax.random.split(key, 4)
        x = jax.random.normal(k1, (B, N, D), dtype=jnp.float32)
        adj = jax.random.uniform(k2, (N, N), dtype=jnp.float32)
        weight = jax.random.normal(k3, (D, O), dtype=jnp.float32) * 0.02
        bias = jax.random.normal(k4, (O,), dtype=jnp.float32) * 0.02
        return {'x': x, 'adj': adj, 'weight': weight, 'bias': bias}
    _L0_gnn_all = _L0_gnn_setup()
    _L0_gnn_in = {k: v for k, v in _L0_gnn_all.items() if k in ('weight', 'bias')}
    del _L0_gnn_all

    def _L1_gnn_setup():
        import jax, jax.numpy as jnp
        import numpy as np
        B, N, D = (8, 1024, 256)
        key = jax.random.key(seed)
        k1, k2, k3, k4, k5 = jax.random.split(key, 5)
        neuron_states = jax.random.normal(k1, (B, N, D), dtype=jnp.float32)
        adjacency = jax.random.randint(k2, (N, N), 0, 2).astype(jnp.float32)
        scale = 1.0 / np.sqrt(D)
        Wq = jax.random.normal(k3, (D, D), dtype=jnp.float32) * scale
        Wk = jax.random.normal(k4, (D, D), dtype=jnp.float32) * scale
        Wv = jax.random.normal(k5, (D, D), dtype=jnp.float32) * scale
        return {'neuron_states': neuron_states, 'adjacency': adjacency, 'Wq': Wq, 'Wk': Wk, 'Wv': Wv}
    _L1_gnn_all = _L1_gnn_setup()
    _L1_gnn_in = {k: v for k, v in _L1_gnn_all.items() if k in ('Wq', 'Wk', 'Wv')}
    del _L1_gnn_all
    return {'x': x, 'adj': adj, 'L0_gnn_weight': _L0_gnn_in['weight'], 'L0_gnn_bias': _L0_gnn_in['bias'], 'L1_gnn_Wq': _L1_gnn_in['Wq'], 'L1_gnn_Wk': _L1_gnn_in['Wk'], 'L1_gnn_Wv': _L1_gnn_in['Wv']}

def reference(x, adj, L0_gnn_weight, L0_gnn_bias, L1_gnn_Wq, L1_gnn_Wk, L1_gnn_Wv):
    import jax
    import jax.numpy as jnp

    def _L0_gnn_ref(x, adj, weight, bias):
        import jax, jax.numpy as jnp
        import numpy as np
        B, N, D, O = (8, 2048, 256, 256)
        y = jnp.einsum('nm,bmd->bnd', adj, x)
        out = jnp.einsum('bnd,do->bno', y, weight) + bias
        return out

    def _L1_gnn_ref(neuron_states, adjacency, Wq, Wk, Wv):
        import jax, jax.numpy as jnp
        import numpy as np
        B, N, D = (8, 1024, 256)
        q = jnp.einsum('bnd,ed->bne', neuron_states, Wq)
        k = jnp.einsum('bnd,ed->bne', neuron_states, Wk)
        v = jnp.einsum('bnd,ed->bne', neuron_states, Wv)
        rel = jnp.einsum('bnd,bmd->bnm', q, k)
        rel = adjacency.T[None, :, :] * rel
        rel = rel / jnp.linalg.norm(rel, axis=2, keepdims=True)
        return jnp.einsum('bnm,bmd->bnd', rel, v)
    x = _layernorm(x + _L0_gnn_ref(x, adj, L0_gnn_weight, L0_gnn_bias), axis=-1)
    x = _layernorm(x + _L1_gnn_ref(x, adj, L1_gnn_Wq, L1_gnn_Wk, L1_gnn_Wv), axis=-1)
    return x

_drawn_inputs = setup_inputs


def setup_inputs(seed=0):
    import zlib

    import numpy as np

    out = dict(_drawn_inputs(seed))
    spreads = {}
    factors = {}
    for name, (base, spread) in spreads.items():
        noise = np.random.default_rng([zlib.crc32(name.encode()), seed]).standard_normal(out[name].shape)
        drawn = base * np.exp(spread * noise) if base else spread * noise
        out[name] = jnp.asarray(drawn.astype(out[name].dtype))
    for name, factor in factors.items():
        out[name] = (out[name] * factor).astype(out[name].dtype)
    return out
```

```python
from contextlib import ExitStack

import concourse.bass as bass
from concourse import mybir

P = 128
EPS = 1e-5
RING = 3

ALU = mybir.AluOpType
ACT = mybir.ActivationFunctionType
F32 = mybir.dt.float32
F32R = mybir.dt.float32r



def gnn_two_layers(nc, x, adj, w, bias, wq, wk, wv, out):
    B, N, D = x.shape
    T = N // P
    C = D // P
    assert T == 2 and C == 2 and N == D
    LAST_LAG = 3
    FIRST_TURN = 2
    END_TURN = (B - 1) // RING
    PEELED_HEAD = range(0, RING * FIRST_TURN)
    PEELED_TAIL = range(RING * END_TURN, B + LAST_LAG)

    class Batch:

        def __init__(self, turn, k, lag):
            self.b = RING * turn + (k - lag)
            self.slot = (k - lag) % RING
            self.uses = turn + (k - lag) // RING
            self.fixed = isinstance(turn, int)
            self.runs = not self.fixed or 0 <= self.b < B
            self.bank_reused = not self.fixed or self.b >= 1
            self.slot_reused = not self.fixed or self.b >= RING
            self.first = self.fixed and self.b == 0

    with ExitStack() as ctx:
        def sb(name, shape, dt=F32):
            return ctx.enter_context(nc.sbuf_tensor(name, shape, dt))

        def bank(name):
            return ctx.enter_context(nc.psum_tensor(name, [P, 2, 256], F32))

        def sem(name):
            return ctx.enter_context(nc.semaphore(name))

        def ring(name, shape, dt=F32):
            return [sb(f"{name}{i}", shape, dt) for i in range(RING)]

        ident = sb("ident", [P, P])
        eps = sb("eps", [P, 1])
        adj_in = sb("adj_in", [P, T, N])
        w_in = sb("w_in", [P, C, D])
        wq_in = sb("wq_in", [P, C, D])
        wk_in = sb("wk_in", [P, C, D])
        wv_in = sb("wv_in", [P, C, D])
        bias_in = sb("bias_in", [P, T, D])
        adjT = sb("adjT", [P, T, N])
        adjT_h, adjT_l = sb("adjT_h", [P, T, N], F32R), sb("adjT_l", [P, T, N], F32R)
        w_h, w_l = sb("w_h", [P, C, D], F32R), sb("w_l", [P, C, D], F32R)
        a_h, a_l = sb("a_h", [P, C, D], F32R), sb("a_l", [P, C, D], F32R)
        wvT_h, wvT_l = sb("wvT_h", [P, C, D], F32R), sb("wvT_l", [P, C, D], F32R)

        x_in = ring("x_in", [P, T, D])
        x_h, x_l = ring("x_h", [P, T, D], F32R), ring("x_l", [P, T, D], F32R)
        xb = ring("xb", [P, T, D])
        yT_h, yT_l = ring("yT_h", [P, C, N], F32R), ring("yT_l", [P, C, N], F32R)
        r = ring("r", [P, T, D])
        x1 = ring("x1", [P, T, D])
        x1T_h, x1T_l = ring("x1T_h", [P, C, N], F32R), ring("x1T_l", [P, C, N], F32R)
        gT_h, gT_l = ring("gT_h", [P, C, N], F32R), ring("gT_l", [P, C, N], F32R)
        v_h, v_l = ring("v_h", [P, T, D], F32R), ring("v_l", [P, T, D], F32R)
        s = ring("s", [P, T, N])
        s_sq = ring("s_sq", [P, T, N])
        sT_h, sT_l = ring("sT_h", [P, T, N], F32R), ring("sT_l", [P, T, N], F32R)
        r2 = ring("r2", [P, T, D])
        x2 = ring("x2", [P, T, D])
        st1, st2 = ring("st1", [P, T, 6]), ring("st2", [P, T, 6])
        mv1, mv2 = ring("mv1", [P, T, 2]), ring("mv2", [P, T, 2])
        std1, std2 = ring("std1", [P, T]), ring("std2", [P, T])
        rstd1, rstd2 = ring("rstd1", [P, T]), ring("rstd2", [P, T])
        shift1, shift2 = ring("shift1", [P, T]), ring("shift2", [P, T])
        ssq, norm, inv_norm = ring("ssq", [P, T]), ring("norm", [P, T]), ring("inv_norm", [P, T])

        ps_y, ps_h, ps_x1T, ps_g = bank("ps_y"), bank("ps_h"), bank("ps_x1T"), bank("ps_g")
        ps_v, ps_rel, ps_sT, ps_o = bank("ps_v"), bank("ps_rel"), bank("ps_sT"), bank("ps_o")

        adj_loaded, w_loaded, bias_loaded = sem("adj_loaded"), sem("w_loaded"), sem("bias_loaded")
        wqk_loaded, wv_loaded = sem("wqk_loaded"), sem("wv_loaded")
        x_loaded = [sem(f"x_loaded{i}") for i in range(RING)]
        stored = [sem(f"stored{i}") for i in range(RING)]
        ident_zeroed, ident_ready, eps_ready = sem("ident_zeroed"), sem("ident_ready"), sem("eps_ready")
        adjT_done, adjT_h_ready, adjT_ready = sem("adjT_done"), sem("adjT_h_ready"), sem("adjT_ready")
        w_h_ready, w_ready = sem("w_h_ready"), sem("w_ready")
        a_done, a_h_ready, a_ready = sem("a_done"), sem("a_h_ready"), sem("a_ready")
        wvT_done, wvT_h_ready, wvT_ready = sem("wvT_done"), sem("wvT_h_ready"), sem("wvT_ready")
        y_done, h_done, x1T_done, g_done = sem("y_done"), sem("h_done"), sem("x1T_done"), sem("g_done")
        v_done, rel_done, sT_done, o_done = sem("v_done"), sem("rel_done"), sem("sT_done"), sem("o_done")
        x_h_ready, x_l_ready = sem("x_h_ready"), sem("x_l_ready")
        yT_h_ready, yT_l_ready = sem("yT_h_ready"), sem("yT_l_ready")
        x1T_h_ready, x1T_l_ready = sem("x1T_h_ready"), sem("x1T_l_ready")
        gT_h_ready, gT_l_ready = sem("gT_h_ready"), sem("gT_l_ready")
        v_h_ready, v_l_ready = sem("v_h_ready"), sem("v_l_ready")
        sT_h_ready, sT_l_ready = sem("sT_h_ready"), sem("sT_l_ready")
        xb_ready, r_ready, s_ready, ssq_ready = sem("xb_ready"), sem("r_ready"), sem("s_ready"), sem("ssq_ready")
        norm_ready, inv_norm_ready = sem("norm_ready"), sem("inv_norm_ready")
        r2_halves, x1_ready, x2_halves = sem("r2_halves"), sem("x1_ready"), sem("x2_halves")
        st1_halves, st2_halves, mv1_ready, mv2_ready = sem("st1_halves"), sem("st2_halves"), sem("mv1_ready"), sem("mv2_ready")
        std1_ready, std2_ready, rstd1_ready, rstd2_ready = sem("std1_ready"), sem("std2_ready"), sem("rstd1_ready"), sem("rstd2_ready")
        shift1_ready, shift2_ready = sem("shift1_ready"), sem("shift2_ready")

        x_v = x.rearrange("b (p t) d -> b p t d", t=T)
        out_v = out.rearrange("b (p t) d -> b p t d", t=T)

        block = ctx.enter_context(nc.Block())

        @block.sync
        def _(sp):
            sp.dma_start(adj_in[:], adj.rearrange("(p t) m -> p t m", t=T)).then_inc(adj_loaded, 16)

            def load_x(turn, k):
                b = Batch(turn, k, -2)
                if b.runs:
                    if b.slot_reused:
                        sp.wait_ge(x_h_ready, b.b - RING + 1)
                        sp.wait_ge(x_l_ready, b.b - RING + 1)
                        sp.wait_ge(xb_ready, b.b - RING + 1)
                    sp.dma_start(x_in[b.slot][:], x_v[b.b]).then_inc(x_loaded[b.slot], 16)

            def store(turn, k):
                b = Batch(turn, k, 3)
                if b.runs:
                    sp.wait_ge(x2_halves, 2 * b.b + 2)
                    sp.dma_start(out_v[b.b], x2[b.slot][:]).then_inc(stored[b.slot], 16)

            load_x(-1, 1)
            sp.dma_start(w_in[:], w.rearrange("(c p) o -> p c o", p=P)).then_inc(w_loaded, 16)
            load_x(-1, 2)
            sp.dma_start(wq_in[:], wq.rearrange("(p c) d -> p c d", c=C)).then_inc(wqk_loaded, 16)
            sp.dma_start(wk_in[:], wk.rearrange("(p c) d -> p c d", c=C)).then_inc(wqk_loaded, 16)
            sp.dma_start(wv_in[:], wv.rearrange("(c p) d -> p c d", p=P)).then_inc(wv_loaded, 16)
            for i in PEELED_HEAD:
                load_x(i // RING, i % RING)
                store(i // RING, i % RING)
            with sp.Fori(FIRST_TURN, END_TURN) as turn:
                for k in range(RING):
                    load_x(turn, k)
                    store(turn, k)
            for i in PEELED_TAIL:
                load_x(i // RING, i % RING)
                store(i // RING, i % RING)
            for slot in range(RING):
                sp.wait_ge(stored[slot], 16 * len(range(slot, B, RING)))

        @block.tensor
        def _(pe):
            def product(bank_, stat_h, stat_l, mov_h, mov_l, wait_hi, wait_lo):
                wait_hi()
                for j in range(2):
                    cut = slice(j * P, (j + 1) * P)
                    for c in range(2):
                        nc.tensor.matmul(bank_[:, j], stat_h[:, c, cut], mov_h[:, c], start=(c == 0), stop=False)
                    if j == 0:
                        wait_lo()
                    for c in range(2):
                        nc.tensor.matmul(bank_[:, j], stat_h[:, c, cut], mov_l[:, c], start=False, stop=False)
                    for c in range(2):
                        last = nc.tensor.matmul(bank_[:, j], stat_l[:, c, cut], mov_h[:, c], start=False, stop=(c == 1))
                return last

            def step(turn, k):
                b = Batch(turn, k, 0)
                if b.runs:
                    if b.bank_reused:
                        pe.wait_ge(yT_l_ready, b.b)
                    product(ps_y, x_h[b.slot], x_l[b.slot], adjT_h, adjT_l,
                            lambda: pe.wait_ge(x_h_ready, b.b + 1),
                            lambda: pe.wait_ge(x_l_ready, b.b + 1)).then_inc(y_done, 1)
                b = Batch(turn, k, 1)
                if b.runs:
                    pe.wait_ge(x1_ready, b.b + 1)
                    if b.bank_reused:
                        pe.wait_ge(x1T_l_ready, b.b)
                    for c in range(C):
                        for t in range(T):
                            last = nc.tensor.transpose(ps_x1T[:, c, t * P:(t + 1) * P],
                                                       x1[b.slot][:, t, c * P:(c + 1) * P], ident[:])
                    last.then_inc(x1T_done, 1)
                b = Batch(turn, k, 2)
                if b.runs:
                    if b.bank_reused:
                        pe.wait_ge(s_ready, b.b)
                    product(ps_rel, gT_h[b.slot], gT_l[b.slot], x1T_h[b.slot], x1T_l[b.slot],
                            lambda: pe.wait_ge(gT_h_ready, b.b + 1),
                            lambda: pe.wait_ge(gT_l_ready, b.b + 1)).then_inc(rel_done, 1)
                b = Batch(turn, k, 0)
                if b.runs:
                    if b.first:
                        pe.wait_ge(w_ready, 1)
                    if b.bank_reused:
                        pe.wait_ge(r_ready, b.b)
                    product(ps_h, yT_h[b.slot], yT_l[b.slot], w_h, w_l,
                            lambda: pe.wait_ge(yT_h_ready, b.b + 1),
                            lambda: pe.wait_ge(yT_l_ready, b.b + 1)).then_inc(h_done, 1)
                b = Batch(turn, k, 2)
                if b.runs:
                    pe.wait_ge(s_ready, b.b + 1)
                    if b.bank_reused:
                        pe.wait_ge(sT_l_ready, b.b)
                    for u in range(T):
                        for t in range(T):
                            last = nc.tensor.transpose(ps_sT[:, u, t * P:(t + 1) * P],
                                                       s[b.slot][:, t, u * P:(u + 1) * P], ident[:])
                    last.then_inc(sT_done, 1)
                b = Batch(turn, k, 1)
                if b.runs:
                    if b.bank_reused:
                        pe.wait_ge(gT_l_ready, b.b)
                    product(ps_g, a_h, a_l, x1T_h[b.slot], x1T_l[b.slot],
                            lambda: pe.wait_ge(x1T_h_ready, b.b + 1),
                            lambda: pe.wait_ge(x1T_l_ready, b.b + 1)).then_inc(g_done, 1)
                    if b.bank_reused:
                        pe.wait_ge(v_l_ready, b.b)
                    product(ps_v, x1T_h[b.slot], x1T_l[b.slot], wvT_h, wvT_l,
                            lambda: pe.wait_ge(x1T_h_ready, b.b + 1),
                            lambda: pe.wait_ge(x1T_l_ready, b.b + 1)).then_inc(v_done, 1)
                b = Batch(turn, k, 2)
                if b.runs:
                    pe.wait_ge(v_l_ready, b.b + 1)
                    if b.bank_reused:
                        pe.wait_ge(r2_halves, 2 * b.b)
                    product(ps_o, sT_h[b.slot], sT_l[b.slot], v_h[b.slot], v_l[b.slot],
                            lambda: pe.wait_ge(sT_h_ready, b.b + 1),
                            lambda: pe.wait_ge(sT_l_ready, b.b + 1)).then_inc(o_done, 1)

            pe.wait_ge(ident_ready, 1)
            pe.wait_ge(adj_loaded, 16)
            for u in range(T):
                for t in range(T):
                    last = nc.tensor.transpose(ps_sT[:, u, t * P:(t + 1) * P],
                                               adj_in[:, t, u::T], ident[:])
            last.then_inc(adjT_done, 1)
            pe.wait_ge(adjT_ready, 1)
            step(0, 0)
            pe.wait_ge(wqk_loaded, 32)
            for j in range(C):
                for c in range(C):
                    last = nc.tensor.matmul(ps_g[:, j], wq_in[:, c, j * P:(j + 1) * P], wk_in[:, c],
                                            start=(c == 0), stop=(c == C - 1))
            last.then_inc(a_done, 1)
            pe.wait_ge(wv_loaded, 16)
            for c in range(C):
                for e in range(C):
                    last = nc.tensor.transpose(ps_v[:, c, e * P:(e + 1) * P],
                                               wv_in[:, e, c * P:(c + 1) * P], ident[:])
            last.then_inc(wvT_done, 1)
            pe.wait_ge(a_ready, 1)
            pe.wait_ge(wvT_ready, 1)
            for i in PEELED_HEAD[1:]:
                step(i // RING, i % RING)
            with pe.Fori(FIRST_TURN, END_TURN) as turn:
                for k in range(RING):
                    step(turn, k)
            for i in PEELED_TAIL:
                step(i // RING, i % RING)

        @block.scalar
        def _(act):
            def step(turn, k):
                b = Batch(turn, k, 0)
                if b.runs:
                    act.wait_ge(y_done, b.b + 1)
                    if b.slot_reused:
                        act.wait_ge(h_done, b.b - RING + 1)
                    nc.scalar.copy(yT_h[b.slot][:], ps_y[:]).then_inc(yT_h_ready, 1)
                b = Batch(turn, k, 1)
                if b.runs:
                    act.wait_ge(x1T_done, b.b + 1)
                    if b.slot_reused:
                        act.wait_ge(rel_done, b.b - RING + 1)
                    nc.scalar.copy(x1T_h[b.slot][:], ps_x1T[:]).then_inc(x1T_h_ready, 1)
                b = Batch(turn, k, 3)
                if b.runs:
                    act.wait_ge(mv2_ready, 2 * b.b + 2)
                    nc.scalar.activation(std2[b.slot][:], mv2[b.slot][:, :, 1], ACT.Sqrt,
                                         bias=eps[:, 0:1]).then_inc(std2_ready, 1)
                b = Batch(turn, k, -1)
                if b.runs:
                    act.wait_ge(x_loaded[b.slot], 16 * b.uses + 16)
                    if b.slot_reused:
                        act.wait_ge(y_done, b.b - RING + 1)
                    nc.scalar.copy(x_h[b.slot][:], x_in[b.slot][:]).then_inc(x_h_ready, 1)
                b = Batch(turn, k, 2)
                if b.runs:
                    act.wait_ge(s_ready, b.b + 1)
                    for t in range(T):
                        last = nc.scalar.activation(s_sq[b.slot][:, t], s[b.slot][:, t], ACT.Square,
                                                    accum_out=ssq[b.slot][:, t:t + 1])
                    last.then_inc(ssq_ready, 1)
                    act.wait_ge(sT_done, b.b + 1)
                    if b.slot_reused:
                        act.wait_ge(o_done, b.b - RING + 1)
                    nc.scalar.copy(sT_h[b.slot][:], ps_sT[:]).then_inc(sT_h_ready, 1)
                    act.wait_ge(ssq_ready, b.b + 1)
                    nc.scalar.activation(norm[b.slot][:], ssq[b.slot][:], ACT.Sqrt).then_inc(norm_ready, 1)
                b = Batch(turn, k, 1)
                if b.runs:
                    act.wait_ge(g_done, b.b + 1)
                    if b.slot_reused:
                        act.wait_ge(rel_done, b.b - RING + 1)
                    nc.scalar.copy(gT_h[b.slot][:], ps_g[:]).then_inc(gT_h_ready, 1)
                b = Batch(turn, k, 0)
                if b.runs:
                    if b.first:
                        act.wait_ge(eps_ready, 1)
                    act.wait_ge(mv1_ready, 2 * b.b + 2)
                    nc.scalar.activation(std1[b.slot][:], mv1[b.slot][:, :, 1], ACT.Sqrt,
                                         bias=eps[:, 0:1]).then_inc(std1_ready, 1)
                b = Batch(turn, k, 1)
                if b.runs:
                    act.wait_ge(v_done, b.b + 1)
                    if b.slot_reused:
                        act.wait_ge(o_done, b.b - RING + 1)
                    nc.scalar.copy(v_h[b.slot][:], ps_v[:]).then_inc(v_h_ready, 1)
                b = Batch(turn, k, 0)
                if b.runs:
                    act.wait_ge(shift1_ready, b.b + 1)
                    if b.slot_reused:
                        act.wait_ge(r2_halves, 2 * (b.b - RING) + 2)
                    for t in range(T):
                        last = nc.scalar.activation(x1[b.slot][:, t], r[b.slot][:, t], ACT.Identity,
                                                    bias=shift1[b.slot][:, t:t + 1],
                                                    scale=rstd1[b.slot][:, t:t + 1])
                    last.then_inc(x1_ready, 1)

            act.dma_start(bias_in[:], bias.partition_broadcast(P).rearrange("p (a d) -> p a d", a=1)
                          .to_broadcast([P, T, D])).then_inc(bias_loaded, 16)
            act.wait_ge(adjT_done, 1)
            nc.scalar.copy(adjT_h[:], ps_sT[:]).then_inc(adjT_h_ready, 1)
            step(-1, 2)
            act.wait_ge(w_loaded, 16)
            nc.scalar.copy(w_h[:], w_in[:]).then_inc(w_h_ready, 1)
            step(0, 0)
            act.wait_ge(a_done, 1)
            nc.scalar.copy(a_h[:], ps_g[:]).then_inc(a_h_ready, 1)
            act.wait_ge(wvT_done, 1)
            nc.scalar.copy(wvT_h[:], ps_v[:]).then_inc(wvT_h_ready, 1)
            for i in PEELED_HEAD[1:]:
                step(i // RING, i % RING)
            with act.Fori(FIRST_TURN, END_TURN) as turn:
                for k in range(RING):
                    step(turn, k)
            for i in PEELED_TAIL:
                step(i // RING, i % RING)

        @block.vector
        def _(dve):
            def lo_part(dst, value, hi):
                return nc.vector.tensor_tensor(dst[:], value[:], hi[:].bitcast(F32), ALU.subtract)

            def step(turn, k):
                b = Batch(turn, k, 3)
                if b.runs:
                    dve.wait_ge(o_done, b.b + 1)
                    dve.wait_ge(inv_norm_ready, b.b + 1)
                    if b.slot_reused:
                        dve.wait_ge(x2_halves, 2 * (b.b - RING) + 2)
                    for t in range(T):
                        nc.vector.scalar_tensor_tensor(r2[b.slot][:, t], ps_o[:, t], inv_norm[b.slot][:, t:t + 1],
                                                       x1[b.slot][:, t], ALU.mult, ALU.add).then_inc(r2_halves, 1)
                    for t in range(T):
                        dve.wait_ge(r2_halves, 2 * b.b + 1 + t)
                        nc.vector.bn_stats(st2[b.slot][:, t], r2[b.slot][:, t]).then_inc(st2_halves, 1)
                    dve.wait_ge(st2_halves, 2 * b.b + 2)
                b = Batch(turn, k, 0)
                if b.runs:
                    dve.wait_ge(yT_h_ready, b.b + 1)
                    if b.slot_reused:
                        dve.wait_ge(h_done, b.b - RING + 1)
                    lo_part(yT_l[b.slot], ps_y, yT_h[b.slot]).then_inc(yT_l_ready, 1)
                b = Batch(turn, k, 3)
                if b.runs:
                    for t in range(T):
                        nc.vector.bn_aggr(mv2[b.slot][:, t], st2[b.slot][:, t]).then_inc(mv2_ready, 1)
                b = Batch(turn, k, 1)
                if b.runs:
                    dve.wait_ge(x1T_h_ready, b.b + 1)
                    if b.slot_reused:
                        dve.wait_ge(rel_done, b.b - RING + 1)
                    lo_part(x1T_l[b.slot], ps_x1T, x1T_h[b.slot]).then_inc(x1T_l_ready, 1)
                b = Batch(turn, k, 3)
                if b.runs:
                    dve.wait_ge(std2_ready, b.b + 1)
                    nc.vector.reciprocal(rstd2[b.slot][:], std2[b.slot][:]).then_inc(rstd2_ready, 1)
                    dve.wait_ge(rstd2_ready, b.b + 1)
                    nc.vector.scalar_tensor_tensor(shift2[b.slot][:], mv2[b.slot][:, :, 0], -1.0, rstd2[b.slot][:],
                                                   ALU.mult, ALU.mult).then_inc(shift2_ready, 1)
                b = Batch(turn, k, 2)
                if b.runs:
                    dve.wait_ge(rel_done, b.b + 1)
                    if b.slot_reused:
                        dve.wait_ge(sT_done, b.b - RING + 1)
                        dve.wait_ge(ssq_ready, b.b - RING + 1)
                    nc.vector.tensor_tensor(s[b.slot][:], ps_rel[:], adjT[:], ALU.mult).then_inc(s_ready, 1)
                    dve.wait_ge(v_h_ready, b.b + 1)
                    if b.slot_reused:
                        dve.wait_ge(o_done, b.b - RING + 1)
                    lo_part(v_l[b.slot], ps_v, v_h[b.slot]).then_inc(v_l_ready, 1)
                b = Batch(turn, k, 0)
                if b.runs:
                    dve.wait_ge(h_done, b.b + 1)
                    dve.wait_ge(xb_ready, b.b + 1)
                    if b.slot_reused:
                        dve.wait_ge(x1_ready, b.b - RING + 1)
                    nc.vector.tensor_tensor(r[b.slot][:], ps_h[:], xb[b.slot][:], ALU.add).then_inc(r_ready, 1)
                b = Batch(turn, k, 2)
                if b.runs:
                    dve.wait_ge(sT_h_ready, b.b + 1)
                    if b.slot_reused:
                        dve.wait_ge(o_done, b.b - RING + 1)
                    lo_part(sT_l[b.slot], ps_sT, sT_h[b.slot]).then_inc(sT_l_ready, 1)
                b = Batch(turn, k, 0)
                if b.runs:
                    dve.wait_ge(r_ready, b.b + 1)
                    for t in range(T):
                        nc.vector.bn_stats(st1[b.slot][:, t], r[b.slot][:, t]).then_inc(st1_halves, 1)
                    dve.wait_ge(st1_halves, 2 * b.b + 2)
                b = Batch(turn, k, 2)
                if b.runs:
                    dve.wait_ge(norm_ready, b.b + 1)
                    nc.vector.reciprocal(inv_norm[b.slot][:], norm[b.slot][:]).then_inc(inv_norm_ready, 1)
                b = Batch(turn, k, 0)
                if b.runs:
                    for t in range(T):
                        nc.vector.bn_aggr(mv1[b.slot][:, t], st1[b.slot][:, t]).then_inc(mv1_ready, 1)
                b = Batch(turn, k, 1)
                if b.runs:
                    dve.wait_ge(gT_h_ready, b.b + 1)
                    if b.slot_reused:
                        dve.wait_ge(rel_done, b.b - RING + 1)
                    lo_part(gT_l[b.slot], ps_g, gT_h[b.slot]).then_inc(gT_l_ready, 1)
                b = Batch(turn, k, 0)
                if b.runs:
                    dve.wait_ge(std1_ready, b.b + 1)
                    nc.vector.reciprocal(rstd1[b.slot][:], std1[b.slot][:]).then_inc(rstd1_ready, 1)
                    dve.wait_ge(rstd1_ready, b.b + 1)
                    nc.vector.scalar_tensor_tensor(shift1[b.slot][:], mv1[b.slot][:, :, 0], -1.0, rstd1[b.slot][:],
                                                   ALU.mult, ALU.mult).then_inc(shift1_ready, 1)

            nc.vector.memset(eps[:], EPS).then_inc(eps_ready, 1)
            dve.wait_ge(adjT_h_ready, 1)
            lo_part(adjT_l, ps_sT, adjT_h).then_inc(adjT_ready, 1)
            nc.vector.tensor_copy(adjT[:], ps_sT[:]).then_inc(adjT_ready, 1)
            dve.wait_ge(w_h_ready, 1)
            lo_part(w_l, w_in, w_h).then_inc(w_ready, 1)
            step(0, 0)
            dve.wait_ge(a_h_ready, 1)
            lo_part(a_l, ps_g, a_h).then_inc(a_ready, 1)
            dve.wait_ge(wvT_h_ready, 1)
            lo_part(wvT_l, ps_v, wvT_h).then_inc(wvT_ready, 1)
            for i in PEELED_HEAD[1:]:
                step(i // RING, i % RING)
            with dve.Fori(FIRST_TURN, END_TURN) as turn:
                for k in range(RING):
                    step(turn, k)
            for i in PEELED_TAIL:
                step(i // RING, i % RING)

        @block.gpsimd
        def _(pool):
            def step(turn, k):
                b = Batch(turn, k, -1)
                if b.runs:
                    pool.wait_ge(x_h_ready, b.b + 1)
                    if b.slot_reused:
                        pool.wait_ge(y_done, b.b - RING + 1)
                    nc.gpsimd.tensor_tensor(x_l[b.slot][:], x_in[b.slot][:], x_h[b.slot][:].bitcast(F32),
                                            ALU.subtract).then_inc(x_l_ready, 1)
                    if b.slot_reused:
                        pool.wait_ge(r_ready, b.b - RING + 1)
                b = Batch(turn, k, 3)
                if b.runs:
                    pool.wait_ge(shift2_ready, b.b + 1)
                    if b.slot_reused:
                        pool.wait_ge(stored[b.slot], 16 * b.uses)
                b = Batch(turn, k, -1)
                if b.runs:
                    nc.gpsimd.tensor_tensor(xb[b.slot][:], x_in[b.slot][:], bias_in[:], ALU.add).then_inc(xb_ready, 1)
                b = Batch(turn, k, 3)
                if b.runs:
                    for t in range(T):
                        nc.gpsimd.tensor_scalar(x2[b.slot][:, t], r2[b.slot][:, t], rstd2[b.slot][:, t:t + 1],
                                                shift2[b.slot][:, t:t + 1], ALU.mult, ALU.add).then_inc(x2_halves, 1)

            nc.gpsimd.memset(ident[:], 0.0).then_inc(ident_zeroed, 1)
            pool.wait_ge(ident_zeroed, 1)
            nc.gpsimd.affine_select(out=ident[:], in_=ident[:], compare_op=ALU.not_equal, fill=1.0, base=0,
                                    pattern=[[-1, P]], channel_multiplier=1).then_inc(ident_ready, 1)
            pool.wait_ge(bias_loaded, 16)
            step(-1, 2)
            for i in PEELED_HEAD:
                step(i // RING, i % RING)
            with pool.Fori(FIRST_TURN, END_TURN) as turn:
                for k in range(RING):
                    step(turn, k)
            for i in PEELED_TAIL:
                step(i // RING, i % RING)


_INS = ["x", "adj", "L0_gnn_weight", "L0_gnn_bias", "L1_gnn_Wq", "L1_gnn_Wk", "L1_gnn_Wv"]
_OUTS = [((32, 256, 256), "float32")]


def kernel(**inputs):
    import numpy as _np
    import concourse.bacc as _bacc
    from concourse import mybir as _mybir
    from concourse.bass_utils import run_bass_kernel_spmd as _run

    nc = _bacc.Bacc("TRN2", target_bir_lowering=False, num_devices=1)
    arrays, args = {}, []
    for name in _INS:
        a = _np.ascontiguousarray(inputs[name])
        arrays[f"in_{name}_dram"] = a
        args.append(nc.dram_tensor(f"in_{name}_dram", a.shape, _mybir.dt.from_np(a.dtype), kind="ExternalInput").ap())
    for i, (shape, dtype) in enumerate(_OUTS):
        dt = _mybir.dt.from_np(_np.dtype(dtype))
        args.append(nc.dram_tensor(f"out_{i}_dram", shape, dt, kind="ExternalOutput").ap())
    gnn_two_layers(nc, *args)
    got = _run(nc, [arrays], core_ids=[0])
    return got.results[0]["out_0_dram"]
```

```python
from contextlib import ExitStack

import concourse.bass as bass
from concourse import mybir

P = 128
EPS = 1e-5
RING = 3

ALU = mybir.AluOpType
ACT = mybir.ActivationFunctionType
F32 = mybir.dt.float32
F32R = mybir.dt.float32r



def gnn_two_layers(nc, x, adj, w, bias, wq, wk, wv, out):
    B, N, D = x.shape
    T = N // P
    C = D // P
    assert T == 2 and C == 2 and N == D
    LOOP_FIRST = 2 * RING
    LOOP_END = (B - 2) // RING * RING

    class Batch:

        def __init__(self, turn, k, lag=0):
            self.b = RING * turn + (k - lag)
            self.slot = (k - lag) % RING
            self.uses = turn + (k - lag) // RING
            self.fixed = isinstance(turn, int)
            self.bank_reused = not self.fixed or self.b >= 1
            self.slot_reused = not self.fixed or self.b >= RING
            self.first = self.fixed and self.b == 0
            self.last = self.fixed and self.b == B - 1

    def batch(b):
        return Batch(b // RING, b % RING)

    with ExitStack() as ctx:
        def sb(name, shape, dt=F32):
            return ctx.enter_context(nc.sbuf_tensor(name, shape, dt))

        def bank(name):
            return ctx.enter_context(nc.psum_tensor(name, [P, 2, 256], F32))

        def sem(name):
            return ctx.enter_context(nc.semaphore(name))

        def ring(name, shape, dt=F32):
            return [sb(f"{name}{i}", shape, dt) for i in range(RING)]

        ident = sb("ident", [P, P])
        eps, root_of_eps = sb("eps", [P, 1]), sb("root_of_eps", [P, 1])
        adj_in = sb("adj_in", [P, T, N])
        w_in = sb("w_in", [P, C, D])
        wq_in = sb("wq_in", [P, C, D])
        wk_in = sb("wk_in", [P, C, D])
        wv_in = sb("wv_in", [P, C, D])
        bias_in = sb("bias_in", [P, T, D])
        adjT = sb("adjT", [P, T, N])
        adjT_h, adjT_l = sb("adjT_h", [P, T, N], F32R), sb("adjT_l", [P, T, N], F32R)
        w_h, w_l = sb("w_h", [P, C, D], F32R), sb("w_l", [P, C, D], F32R)
        wq_h, wq_l = sb("wq_h", [P, C, D], F32R), sb("wq_l", [P, C, D], F32R)
        wk_h, wk_l = sb("wk_h", [P, C, D], F32R), sb("wk_l", [P, C, D], F32R)
        a_h, a_l = sb("a_h", [P, C, D], F32R), sb("a_l", [P, C, D], F32R)
        wvT_h, wvT_l = sb("wvT_h", [P, C, D], F32R), sb("wvT_l", [P, C, D], F32R)

        x_in = ring("x_in", [P, T, D])
        x_h, x_l = ring("x_h", [P, T, D], F32R), ring("x_l", [P, T, D], F32R)
        xb = ring("xb", [P, T, D])
        yT_h, yT_l = ring("yT_h", [P, C, N], F32R), ring("yT_l", [P, C, N], F32R)
        r = ring("r", [P, T, D])
        x1 = ring("x1", [P, T, D])
        x1T_h, x1T_l = ring("x1T_h", [P, C, N], F32R), ring("x1T_l", [P, C, N], F32R)
        gT_h, gT_l = ring("gT_h", [P, C, N], F32R), ring("gT_l", [P, C, N], F32R)
        v_h, v_l = ring("v_h", [P, T, D], F32R), ring("v_l", [P, T, D], F32R)
        s = ring("s", [P, T, N])
        s_sq = ring("s_sq", [P, T, N])
        sT_h, sT_l = ring("sT_h", [P, T, N], F32R), ring("sT_l", [P, T, N], F32R)
        r2 = ring("r2", [P, T, D])
        x2 = ring("x2", [P, T, D])
        st1, st2 = ring("st1", [P, T, 6]), ring("st2", [P, T, 6])
        mv1, mv2 = ring("mv1", [P, T, 2]), ring("mv2", [P, T, 2])
        std1, std2 = ring("std1", [P, T]), ring("std2", [P, T])
        rstd1, rstd2 = ring("rstd1", [P, T]), ring("rstd2", [P, T])
        shift1, shift2 = ring("shift1", [P, T]), ring("shift2", [P, T])
        ssq, norm, inv_norm = ring("ssq", [P, T]), ring("norm", [P, T]), ring("inv_norm", [P, T])

        ps_y, ps_h, ps_x1T, ps_g = bank("ps_y"), bank("ps_h"), bank("ps_x1T"), bank("ps_g")
        ps_v, ps_rel, ps_sT, ps_o = bank("ps_v"), bank("ps_rel"), bank("ps_sT"), bank("ps_o")

        adj_loaded, w_loaded, bias_loaded = sem("adj_loaded"), sem("w_loaded"), sem("bias_loaded")
        wqk_loaded, wv_loaded = sem("wqk_loaded"), sem("wv_loaded")
        x_loaded = [sem(f"x_loaded{i}") for i in range(RING)]
        stored = [sem(f"stored{i}") for i in range(RING)]
        ident_zeroed, ident_ready, eps_ready = sem("ident_zeroed"), sem("ident_ready"), sem("eps_ready")
        adjT_done, adjT_ready = sem("adjT_done"), sem("adjT_ready")
        adjT_h_ready, adjT_l_ready = sem("adjT_h_ready"), sem("adjT_l_ready")
        w_h_ready, w_l_ready = sem("w_h_ready"), sem("w_l_ready")
        wqk_h_ready, wqk_l_ready = sem("wqk_h_ready"), sem("wqk_l_ready")
        a_done, a_h_ready, a_l_ready = sem("a_done"), sem("a_h_ready"), sem("a_l_ready")
        wvT_done, wvT_h_ready, wvT_l_ready = sem("wvT_done"), sem("wvT_h_ready"), sem("wvT_l_ready")
        y_done, h_done, x1T_done, g_done = sem("y_done"), sem("h_done"), sem("x1T_done"), sem("g_done")
        v_done, rel_done, sT_done, o_done = sem("v_done"), sem("rel_done"), sem("sT_done"), sem("o_done")
        x_h_ready, x_l_ready = sem("x_h_ready"), sem("x_l_ready")
        yT_h_ready, yT_l_ready = sem("yT_h_ready"), sem("yT_l_ready")
        x1T_h_ready, x1T_l_ready = sem("x1T_h_ready"), sem("x1T_l_ready")
        gT_h_ready, gT_l_ready = sem("gT_h_ready"), sem("gT_l_ready")
        v_h_ready, v_l_ready = sem("v_h_ready"), sem("v_l_ready")
        sT_h_ready, sT_l_ready = sem("sT_h_ready"), sem("sT_l_ready")
        xb_ready, r_ready, s_ready, ssq_ready = sem("xb_ready"), sem("r_ready"), sem("s_ready"), sem("ssq_ready")
        norm_ready, inv_norm_ready = sem("norm_ready"), sem("inv_norm_ready")
        r2_halves, x1_ready, x2_halves = sem("r2_halves"), sem("x1_ready"), sem("x2_halves")
        last_halves = sem("last_halves")
        st1_halves, st2_halves, mv1_ready, mv2_ready = sem("st1_halves"), sem("st2_halves"), sem("mv1_ready"), sem("mv2_ready")
        std1_ready, std2_ready, rstd1_ready, rstd2_ready = sem("std1_ready"), sem("std2_ready"), sem("rstd1_ready"), sem("rstd2_ready")
        shift1_ready, shift2_ready = sem("shift1_ready"), sem("shift2_ready")

        x_v = x.rearrange("b (p t) d -> b p t d", t=T)
        out_v = out.rearrange("b (p t) d -> b p t d", t=T)

        block = ctx.enter_context(nc.Block())

        @block.sync
        def _(sp):
            def load_x(b):
                if b.slot_reused:
                    sp.wait_ge(x_h_ready, b.b - RING + 1)
                    sp.wait_ge(x_l_ready, b.b - RING + 1)
                    sp.wait_ge(xb_ready, b.b - RING + 1)
                sp.dma_start(x_in[b.slot][:], x_v[b.b]).then_inc(x_loaded[b.slot], 16)

            def store(b):
                if b.last:
                    sp.wait_ge(last_halves, 2)
                else:
                    sp.wait_ge(x2_halves, 2 * b.b + 2)
                sp.dma_start(out_v[b.b], x2[b.slot][:]).then_inc(stored[b.slot], 16)

            sp.dma_start(adj_in[:], adj.rearrange("(p t) m -> p t m", t=T)).then_inc(adj_loaded, 16)
            sp.dma_start(w_in[:], w.rearrange("(c p) o -> p c o", p=P)).then_inc(w_loaded, 16)
            load_x(batch(1))
            sp.dma_start(wv_in[:], wv.rearrange("(c p) d -> p c d", p=P)).then_inc(wv_loaded, 16)
            sp.dma_start(wq_in[:], wq.rearrange("(p c) d -> p c d", c=C)).then_inc(wqk_loaded, 16)
            sp.dma_start(wk_in[:], wk.rearrange("(p c) d -> p c d", c=C)).then_inc(wqk_loaded, 16)
            for i in range(2, 5):
                load_x(batch(i))
            for i in range(3, LOOP_FIRST):
                load_x(batch(i + 2))
                store(batch(i - 3))
            with sp.Fori(LOOP_FIRST // RING, LOOP_END // RING) as turn:
                for k in range(RING):
                    load_x(Batch(turn, k, -2))
                    store(Batch(turn, k, 3))
            for i in range(LOOP_END - 3, B):
                if i + 5 < B:
                    load_x(batch(i + 5))
                store(batch(i))
            for slot in range(RING):
                sp.wait_ge(stored[slot], 16 * len(range(slot, B, RING)))

        @block.tensor
        def _(pe):
            def product(result, stat_h, stat_l, mov_h, mov_l, await_lo=None):
                for j in range(2):
                    cut = slice(j * P, (j + 1) * P)
                    for c in range(2):
                        nc.tensor.matmul(result[:, j], stat_h[:, c, cut], mov_h[:, c], start=(c == 0), stop=False)
                    if j == 0 and await_lo:
                        await_lo()
                    for c in range(2):
                        nc.tensor.matmul(result[:, j], stat_h[:, c, cut], mov_l[:, c], start=False, stop=False)
                    for c in range(2):
                        last = nc.tensor.matmul(result[:, j], stat_l[:, c, cut], mov_h[:, c], start=False, stop=(c == 1))
                return last

            def transposed(result, value):
                for c in range(2):
                    for t in range(2):
                        last = nc.tensor.transpose(result[:, c, t * P:(t + 1) * P],
                                                   value[:, t, c * P:(c + 1) * P], ident[:])
                return last

            def y_product(b):
                if b.bank_reused:
                    pe.wait_ge(yT_l_ready, b.b)
                pe.wait_ge(x_h_ready, b.b + 1)
                if b.first:
                    pe.wait_ge(adjT_h_ready, 1)

                def await_lo():
                    if b.first:
                        pe.wait_ge(adjT_l_ready, 1)
                    pe.wait_ge(x_l_ready, b.b + 1)
                product(ps_y, x_h[b.slot], x_l[b.slot], adjT_h, adjT_l, await_lo).then_inc(y_done, 1)

            def h_product(b):
                if b.first:
                    pe.wait_ge(w_l_ready, 1)
                if b.bank_reused:
                    pe.wait_ge(r_ready, b.b)
                pe.wait_ge(yT_h_ready, b.b + 1)
                product(ps_h, yT_h[b.slot], yT_l[b.slot], w_h, w_l,
                        lambda: pe.wait_ge(yT_l_ready, b.b + 1)).then_inc(h_done, 1)

            def x1_transpose(b):
                if b.bank_reused:
                    pe.wait_ge(x1T_l_ready, b.b)
                pe.wait_ge(x1_ready, b.b + 1)
                transposed(ps_x1T, x1[b.slot]).then_inc(x1T_done, 1)

            def g_product(b):
                if b.first:
                    pe.wait_ge(a_l_ready, 1)
                if b.bank_reused:
                    pe.wait_ge(gT_l_ready, b.b)
                pe.wait_ge(x1T_h_ready, b.b + 1)
                product(ps_g, a_h, a_l, x1T_h[b.slot], x1T_l[b.slot],
                        lambda: pe.wait_ge(x1T_l_ready, b.b + 1)).then_inc(g_done, 1)

            def v_product(b):
                if b.first:
                    pe.wait_ge(wvT_l_ready, 1)
                if b.bank_reused:
                    pe.wait_ge(v_l_ready, b.b)
                product(ps_v, x1T_h[b.slot], x1T_l[b.slot], wvT_h, wvT_l).then_inc(v_done, 1)

            def rel_product(b):
                if b.bank_reused:
                    pe.wait_ge(s_ready, b.b)
                pe.wait_ge(gT_h_ready, b.b + 1)
                product(ps_rel, gT_h[b.slot], gT_l[b.slot], x1T_h[b.slot], x1T_l[b.slot],
                        lambda: pe.wait_ge(gT_l_ready, b.b + 1)).then_inc(rel_done, 1)

            def s_transpose(b):
                if b.bank_reused:
                    pe.wait_ge(sT_l_ready, b.b)
                pe.wait_ge(s_ready, b.b + 1)
                transposed(ps_sT, s[b.slot]).then_inc(sT_done, 1)

            def o_product(b):
                if b.bank_reused:
                    pe.wait_ge(r2_halves, 2 * b.b)
                pe.wait_ge(v_l_ready, b.b + 1)
                pe.wait_ge(sT_h_ready, b.b + 1)
                product(ps_o, sT_h[b.slot], sT_l[b.slot], v_h[b.slot], v_l[b.slot],
                        lambda: pe.wait_ge(sT_l_ready, b.b + 1)).then_inc(o_done, 1)

            def step(b0, b1, b2):
                y_product(b0)
                x1_transpose(b1)
                rel_product(b2)
                h_product(b0)
                s_transpose(b2)
                g_product(b1)
                v_product(b1)
                o_product(b2)

            pe.wait_ge(ident_ready, 1)
            pe.wait_ge(adj_loaded, 16)
            for u in range(T):
                for t in range(T):
                    last = nc.tensor.transpose(ps_sT[:, u, t * P:(t + 1) * P], adj_in[:, t, u::T], ident[:])
            last.then_inc(adjT_done, 1)
            y_product(batch(0))
            pe.wait_ge(wv_loaded, 16)
            transposed(ps_v, wv_in).then_inc(wvT_done, 1)
            h_product(batch(0))
            y_product(batch(1))
            pe.wait_ge(wqk_l_ready, 2)
            product(ps_g, wq_h, wq_l, wk_h, wk_l).then_inc(a_done, 1)
            h_product(batch(1))
            x1_transpose(batch(0))
            y_product(batch(2))
            g_product(batch(0))
            v_product(batch(0))
            x1_transpose(batch(1))
            rel_product(batch(0))
            h_product(batch(2))
            s_transpose(batch(0))
            g_product(batch(1))
            v_product(batch(1))
            o_product(batch(0))
            for i in range(3, LOOP_FIRST):
                step(batch(i), batch(i - 1), batch(i - 2))
            with pe.Fori(LOOP_FIRST // RING, LOOP_END // RING) as turn:
                for k in range(RING):
                    step(Batch(turn, k), Batch(turn, k, 1), Batch(turn, k, 2))
            for i in range(LOOP_END, B):
                step(batch(i), batch(i - 1), batch(i - 2))
            rel_product(batch(B - 2))
            x1_transpose(batch(B - 1))
            s_transpose(batch(B - 2))
            g_product(batch(B - 1))
            v_product(batch(B - 1))
            rel_product(batch(B - 1))
            o_product(batch(B - 2))
            s_transpose(batch(B - 1))
            o_product(batch(B - 1))

        @block.scalar
        def _(act):
            def x_hi(b):
                act.wait_ge(x_loaded[b.slot], 16 * b.uses + 16)
                if b.slot_reused:
                    act.wait_ge(y_done, b.b - RING + 1)
                nc.scalar.copy(x_h[b.slot][:], x_in[b.slot][:]).then_inc(x_h_ready, 1)

            def y_hi(b):
                act.wait_ge(y_done, b.b + 1)
                if b.slot_reused:
                    act.wait_ge(h_done, b.b - RING + 1)
                nc.scalar.copy(yT_h[b.slot][:], ps_y[:]).then_inc(yT_h_ready, 1)

            def std_1(b):
                act.wait_ge(mv1_ready, 2 * b.b + 2)
                nc.scalar.activation(std1[b.slot][:], mv1[b.slot][:, :, 1], ACT.Sqrt,
                                     bias=eps[:, 0:1]).then_inc(std1_ready, 1)

            def layernorm_1(b):
                act.wait_ge(shift1_ready, b.b + 1)
                if b.slot_reused:
                    act.wait_ge(r2_halves, 2 * (b.b - RING) + 2)
                for t in range(T):
                    last = nc.scalar.activation(x1[b.slot][:, t], r[b.slot][:, t], ACT.Identity,
                                                bias=shift1[b.slot][:, t:t + 1],
                                                scale=rstd1[b.slot][:, t:t + 1])
                last.then_inc(x1_ready, 1)

            def x1T_hi(b):
                act.wait_ge(x1T_done, b.b + 1)
                if b.slot_reused:
                    act.wait_ge(rel_done, b.b - RING + 1)
                nc.scalar.copy(x1T_h[b.slot][:], ps_x1T[:]).then_inc(x1T_h_ready, 1)

            def g_hi(b):
                act.wait_ge(g_done, b.b + 1)
                if b.slot_reused:
                    act.wait_ge(rel_done, b.b - RING + 1)
                nc.scalar.copy(gT_h[b.slot][:], ps_g[:]).then_inc(gT_h_ready, 1)

            def v_hi(b):
                act.wait_ge(v_done, b.b + 1)
                if b.slot_reused:
                    act.wait_ge(o_done, b.b - RING + 1)
                nc.scalar.copy(v_h[b.slot][:], ps_v[:]).then_inc(v_h_ready, 1)

            def square_sums(b):
                act.wait_ge(s_ready, b.b + 1)
                for t in range(T):
                    last = nc.scalar.activation(s_sq[b.slot][:, t], s[b.slot][:, t], ACT.Square,
                                                accum_out=ssq[b.slot][:, t:t + 1])
                last.then_inc(ssq_ready, 1)

            def s_hi(b):
                act.wait_ge(sT_done, b.b + 1)
                if b.slot_reused:
                    act.wait_ge(o_done, b.b - RING + 1)
                nc.scalar.copy(sT_h[b.slot][:], ps_sT[:]).then_inc(sT_h_ready, 1)

            def row_norm(b):
                act.wait_ge(ssq_ready, b.b + 1)
                nc.scalar.activation(norm[b.slot][:], ssq[b.slot][:], ACT.Sqrt).then_inc(norm_ready, 1)

            def std_2(b):
                act.wait_ge(mv2_ready, 2 * b.b + 2)
                nc.scalar.activation(std2[b.slot][:], mv2[b.slot][:, :, 1], ACT.Sqrt,
                                     bias=eps[:, 0:1]).then_inc(std2_ready, 1)

            def step(b_next, b0, b1, b2, b3):
                y_hi(b0)
                x1T_hi(b1)
                std_2(b3)
                x_hi(b_next)
                square_sums(b2)
                s_hi(b2)
                row_norm(b2)
                g_hi(b1)
                std_1(b0)
                v_hi(b1)
                layernorm_1(b0)

            act.dma_start(x_in[0][:], x_v[0]).then_inc(x_loaded[0], 16)
            act.wait_ge(eps_ready, 1)
            nc.scalar.activation(root_of_eps[:], eps[:], ACT.Sqrt)
            x_hi(batch(0))
            act.wait_ge(adjT_done, 1)
            nc.scalar.copy(adjT_h[:], ps_sT[:]).then_inc(adjT_h_ready, 1)
            act.wait_ge(w_loaded, 16)
            nc.scalar.copy(w_h[:], w_in[:]).then_inc(w_h_ready, 1)
            y_hi(batch(0))
            x_hi(batch(1))
            act.wait_ge(wqk_loaded, 32)
            nc.scalar.copy(wq_h[:], wq_in[:]).then_inc(wqk_h_ready, 1)
            nc.scalar.copy(wk_h[:], wk_in[:]).then_inc(wqk_h_ready, 1)
            act.wait_ge(wvT_done, 1)
            nc.scalar.copy(wvT_h[:], ps_v[:]).then_inc(wvT_h_ready, 1)
            x_hi(batch(2))
            y_hi(batch(1))
            std_1(batch(0))
            layernorm_1(batch(0))
            act.wait_ge(a_done, 1)
            nc.scalar.copy(a_h[:], ps_g[:]).then_inc(a_h_ready, 1)
            x1T_hi(batch(0))
            std_1(batch(1))
            y_hi(batch(2))
            x_hi(batch(3))
            layernorm_1(batch(1))
            g_hi(batch(0))
            v_hi(batch(0))
            x1T_hi(batch(1))
            square_sums(batch(0))
            s_hi(batch(0))
            row_norm(batch(0))
            g_hi(batch(1))
            std_1(batch(2))
            v_hi(batch(1))
            layernorm_1(batch(2))
            for i in range(3, LOOP_FIRST):
                step(batch(i + 1), batch(i), batch(i - 1), batch(i - 2), batch(i - 3))
            with act.Fori(LOOP_FIRST // RING, LOOP_END // RING) as turn:
                for k in range(RING):
                    step(*(Batch(turn, k, lag) for lag in range(-1, 4)))
            for i in range(LOOP_END, B - 1):
                step(batch(i + 1), batch(i), batch(i - 1), batch(i - 2), batch(i - 3))
            y_hi(batch(B - 1))
            x1T_hi(batch(B - 2))
            std_2(batch(B - 4))
            square_sums(batch(B - 3))
            s_hi(batch(B - 3))
            row_norm(batch(B - 3))
            std_1(batch(B - 1))
            g_hi(batch(B - 2))
            layernorm_1(batch(B - 1))
            v_hi(batch(B - 2))
            x1T_hi(batch(B - 1))
            s_hi(batch(B - 2))
            std_2(batch(B - 3))
            square_sums(batch(B - 2))
            row_norm(batch(B - 2))
            g_hi(batch(B - 1))
            v_hi(batch(B - 1))
            square_sums(batch(B - 1))
            row_norm(batch(B - 1))
            s_hi(batch(B - 1))
            std_2(batch(B - 2))
            std_2(batch(B - 1))
            last = batch(B - 1)
            act.wait_ge(shift2_ready, B)
            act.wait_ge(stored[last.slot], 16 * last.uses)
            nc.scalar.activation(x2[last.slot][:, 1], r2[last.slot][:, 1], ACT.Identity,
                                 bias=shift2[last.slot][:, 1:2], scale=rstd2[last.slot][:, 1:2]).then_inc(last_halves, 1)

        @block.vector
        def _(dve):
            def lo_part(dst, value, hi):
                return nc.vector.tensor_tensor(dst[:], value[:], hi[:].bitcast(F32), ALU.subtract)

            def y_lo(b):
                dve.wait_ge(yT_h_ready, b.b + 1)
                if b.slot_reused:
                    dve.wait_ge(h_done, b.b - RING + 1)
                lo_part(yT_l[b.slot], ps_y, yT_h[b.slot]).then_inc(yT_l_ready, 1)

            def residual_1(b):
                dve.wait_ge(h_done, b.b + 1)
                dve.wait_ge(xb_ready, b.b + 1)
                if b.slot_reused:
                    dve.wait_ge(x1_ready, b.b - RING + 1)
                nc.vector.tensor_tensor(r[b.slot][:], ps_h[:], xb[b.slot][:], ALU.add).then_inc(r_ready, 1)

            def statistics_1(b):
                dve.wait_ge(r_ready, b.b + 1)
                for t in range(T):
                    nc.vector.bn_stats(st1[b.slot][:, t], r[b.slot][:, t]).then_inc(st1_halves, 1)

            def variance_1(b):
                for t in range(T):
                    nc.vector.bn_aggr(mv1[b.slot][:, t], st1[b.slot][:, t]).then_inc(mv1_ready, 1)

            def scale_and_shift_1(b):
                dve.wait_ge(std1_ready, b.b + 1)
                nc.vector.reciprocal(rstd1[b.slot][:], std1[b.slot][:]).then_inc(rstd1_ready, 1)
                dve.wait_ge(rstd1_ready, b.b + 1)
                nc.vector.scalar_tensor_tensor(shift1[b.slot][:], mv1[b.slot][:, :, 0], -1.0, rstd1[b.slot][:],
                                               ALU.mult, ALU.mult).then_inc(shift1_ready, 1)

            def x1T_lo(b):
                dve.wait_ge(x1T_h_ready, b.b + 1)
                if b.slot_reused:
                    dve.wait_ge(rel_done, b.b - RING + 1)
                lo_part(x1T_l[b.slot], ps_x1T, x1T_h[b.slot]).then_inc(x1T_l_ready, 1)

            def g_lo(b):
                dve.wait_ge(gT_h_ready, b.b + 1)
                if b.slot_reused:
                    dve.wait_ge(rel_done, b.b - RING + 1)
                lo_part(gT_l[b.slot], ps_g, gT_h[b.slot]).then_inc(gT_l_ready, 1)

            def v_lo(b):
                dve.wait_ge(v_h_ready, b.b + 1)
                if b.slot_reused:
                    dve.wait_ge(o_done, b.b - RING + 1)
                lo_part(v_l[b.slot], ps_v, v_h[b.slot]).then_inc(v_l_ready, 1)

            def weigh(b):
                dve.wait_ge(rel_done, b.b + 1)
                if b.slot_reused:
                    dve.wait_ge(sT_done, b.b - RING + 1)
                    dve.wait_ge(ssq_ready, b.b - RING + 1)
                nc.vector.tensor_tensor(s[b.slot][:], ps_rel[:], adjT[:], ALU.mult).then_inc(s_ready, 1)

            def s_lo(b):
                dve.wait_ge(sT_h_ready, b.b + 1)
                if b.slot_reused:
                    dve.wait_ge(o_done, b.b - RING + 1)
                lo_part(sT_l[b.slot], ps_sT, sT_h[b.slot]).then_inc(sT_l_ready, 1)

            def invert_norm(b):
                dve.wait_ge(norm_ready, b.b + 1)
                nc.vector.reciprocal(inv_norm[b.slot][:], norm[b.slot][:]).then_inc(inv_norm_ready, 1)

            def residual_2(b):
                dve.wait_ge(o_done, b.b + 1)
                dve.wait_ge(inv_norm_ready, b.b + 1)
                if b.slot_reused:
                    dve.wait_ge(x2_halves, 2 * (b.b - RING) + 2)
                for t in range(T):
                    nc.vector.scalar_tensor_tensor(r2[b.slot][:, t], ps_o[:, t], inv_norm[b.slot][:, t:t + 1],
                                                   x1[b.slot][:, t], ALU.mult, ALU.add).then_inc(r2_halves, 1)

            def statistics_2(b):
                for t in range(T):
                    dve.wait_ge(r2_halves, 2 * b.b + 1 + t)
                    nc.vector.bn_stats(st2[b.slot][:, t], r2[b.slot][:, t]).then_inc(st2_halves, 1)

            def variance_2(b):
                for t in range(T):
                    nc.vector.bn_aggr(mv2[b.slot][:, t], st2[b.slot][:, t]).then_inc(mv2_ready, 1)

            def scale_2(b):
                dve.wait_ge(std2_ready, b.b + 1)
                nc.vector.reciprocal(rstd2[b.slot][:], std2[b.slot][:]).then_inc(rstd2_ready, 1)

            def shift_2(b):
                dve.wait_ge(rstd2_ready, b.b + 1)
                nc.vector.scalar_tensor_tensor(shift2[b.slot][:], mv2[b.slot][:, :, 0], -1.0, rstd2[b.slot][:],
                                               ALU.mult, ALU.mult).then_inc(shift2_ready, 1)

            def step(b0, b1, b2, b3):
                residual_2(b3)
                statistics_2(b3)
                dve.wait_ge(st2_halves, 2 * b3.b + 2)
                y_lo(b0)
                variance_2(b3)
                x1T_lo(b1)
                weigh(b2)
                scale_2(b3)
                v_lo(b2)
                shift_2(b3)
                residual_1(b0)
                s_lo(b2)
                statistics_1(b0)
                dve.wait_ge(st1_halves, 2 * b0.b + 2)
                invert_norm(b2)
                variance_1(b0)
                g_lo(b1)
                scale_and_shift_1(b0)

            nc.vector.memset(eps[:], EPS).then_inc(eps_ready, 1)
            dve.wait_ge(adjT_h_ready, 1)
            lo_part(adjT_l, ps_sT, adjT_h).then_inc(adjT_l_ready, 1)
            nc.vector.tensor_copy(adjT[:], ps_sT[:]).then_inc(adjT_ready, 1)
            dve.wait_ge(w_h_ready, 1)
            lo_part(w_l, w_in, w_h).then_inc(w_l_ready, 1)
            y_lo(batch(0))
            dve.wait_ge(wqk_h_ready, 1)
            lo_part(wq_l, wq_in, wq_h).then_inc(wqk_l_ready, 1)
            dve.wait_ge(wqk_h_ready, 2)
            lo_part(wk_l, wk_in, wk_h).then_inc(wqk_l_ready, 1)
            residual_1(batch(0))
            statistics_1(batch(0))
            dve.wait_ge(st1_halves, 2)
            variance_1(batch(0))
            y_lo(batch(1))
            scale_and_shift_1(batch(0))
            dve.wait_ge(wvT_h_ready, 1)
            lo_part(wvT_l, ps_v, wvT_h).then_inc(wvT_l_ready, 1)
            dve.wait_ge(a_h_ready, 1)
            lo_part(a_l, ps_g, a_h).then_inc(a_l_ready, 1)
            residual_1(batch(1))
            statistics_1(batch(1))
            x1T_lo(batch(0))
            dve.wait_ge(st1_halves, 4)
            variance_1(batch(1))
            y_lo(batch(2))
            scale_and_shift_1(batch(1))
            g_lo(batch(0))
            v_lo(batch(0))
            x1T_lo(batch(1))
            dve.wait_ge(adjT_ready, 1)
            weigh(batch(0))
            residual_1(batch(2))
            s_lo(batch(0))
            statistics_1(batch(2))
            dve.wait_ge(st1_halves, 6)
            invert_norm(batch(0))
            variance_1(batch(2))
            g_lo(batch(1))
            scale_and_shift_1(batch(2))
            for i in range(3, LOOP_FIRST):
                step(batch(i), batch(i - 1), batch(i - 2), batch(i - 3))
            with dve.Fori(LOOP_FIRST // RING, LOOP_END // RING) as turn:
                for k in range(RING):
                    step(*(Batch(turn, k, lag) for lag in range(4)))
            for i in range(LOOP_END, B):
                step(batch(i), batch(i - 1), batch(i - 2), batch(i - 3))
            residual_2(batch(B - 3))
            statistics_2(batch(B - 3))
            dve.wait_ge(st2_halves, 2 * (B - 3) + 2)
            weigh(batch(B - 2))
            x1T_lo(batch(B - 1))
            variance_2(batch(B - 3))
            s_lo(batch(B - 2))
            v_lo(batch(B - 2))
            scale_2(batch(B - 3))
            invert_norm(batch(B - 2))
            shift_2(batch(B - 3))
            g_lo(batch(B - 1))
            v_lo(batch(B - 1))
            weigh(batch(B - 1))
            residual_2(batch(B - 2))
            invert_norm(batch(B - 1))
            s_lo(batch(B - 1))
            statistics_2(batch(B - 2))
            dve.wait_ge(st2_halves, 2 * (B - 2) + 2)
            variance_2(batch(B - 2))
            scale_2(batch(B - 2))
            shift_2(batch(B - 2))
            residual_2(batch(B - 1))
            statistics_2(batch(B - 1))
            dve.wait_ge(st2_halves, 2 * (B - 1) + 2)
            variance_2(batch(B - 1))
            scale_2(batch(B - 1))
            shift_2(batch(B - 1))
            last = batch(B - 1)
            dve.wait_ge(stored[last.slot], 16 * last.uses)
            dve.wait_ge(shift2_ready, B)
            nc.vector.tensor_scalar(x2[last.slot][:, 0], r2[last.slot][:, 0], rstd2[last.slot][:, 0:1],
                                    shift2[last.slot][:, 0:1], ALU.mult, ALU.add).then_inc(last_halves, 1)

        @block.gpsimd
        def _(pool):
            def x_lo(b):
                pool.wait_ge(x_h_ready, b.b + 1)
                if b.slot_reused:
                    pool.wait_ge(y_done, b.b - RING + 1)
                nc.gpsimd.tensor_tensor(x_l[b.slot][:], x_in[b.slot][:], x_h[b.slot][:].bitcast(F32),
                                        ALU.subtract).then_inc(x_l_ready, 1)

            def add_bias(b):
                if b.slot_reused:
                    pool.wait_ge(r_ready, b.b - RING + 1)
                nc.gpsimd.tensor_tensor(xb[b.slot][:], x_in[b.slot][:], bias_in[:], ALU.add).then_inc(xb_ready, 1)

            def await_layernorm_2(b):
                pool.wait_ge(shift2_ready, b.b + 1)
                if b.slot_reused:
                    pool.wait_ge(stored[b.slot], 16 * b.uses)

            def layernorm_2(b):
                for t in range(T):
                    nc.gpsimd.tensor_scalar(x2[b.slot][:, t], r2[b.slot][:, t], rstd2[b.slot][:, t:t + 1],
                                            shift2[b.slot][:, t:t + 1], ALU.mult, ALU.add).then_inc(x2_halves, 1)

            def step(b_next, b3):
                x_lo(b_next)
                await_layernorm_2(b3)
                add_bias(b_next)
                layernorm_2(b3)

            nc.gpsimd.memset(ident[:], 0.0).then_inc(ident_zeroed, 1)
            pool.wait_ge(ident_zeroed, 1)
            nc.gpsimd.affine_select(out=ident[:], in_=ident[:], compare_op=ALU.not_equal, fill=1.0, base=0,
                                    pattern=[[-1, P]], channel_multiplier=1).then_inc(ident_ready, 1)
            pool.dma_start(bias_in[:], bias.partition_broadcast(P).rearrange("p (a d) -> p a d", a=1)
                           .to_broadcast([P, T, D])).then_inc(bias_loaded, 16)
            x_lo(batch(0))
            pool.wait_ge(bias_loaded, 16)
            add_bias(batch(0))
            for i in range(1, 4):
                x_lo(batch(i))
                add_bias(batch(i))
            for i in range(3, LOOP_FIRST):
                step(batch(i + 1), batch(i - 3))
            with pool.Fori(LOOP_FIRST // RING, LOOP_END // RING) as turn:
                for k in range(RING):
                    step(Batch(turn, k, -1), Batch(turn, k, 3))
            for i in range(LOOP_END, B - 1):
                step(batch(i + 1), batch(i - 3))
            for i in range(B - 1, B + 2):
                await_layernorm_2(batch(i - 3))
                layernorm_2(batch(i - 3))


_INS = ["x", "adj", "L0_gnn_weight", "L0_gnn_bias", "L1_gnn_Wq", "L1_gnn_Wk", "L1_gnn_Wv"]
_OUTS = [((32, 256, 256), "float32")]


def kernel(**inputs):
    import numpy as _np
    import concourse.bacc as _bacc
    from concourse import mybir as _mybir
    from concourse.bass_utils import run_bass_kernel_spmd as _run

    nc = _bacc.Bacc("TRN2", target_bir_lowering=False, num_devices=1)
    arrays, args = {}, []
    for name in _INS:
        a = _np.ascontiguousarray(inputs[name])
        arrays[f"in_{name}_dram"] = a
        args.append(nc.dram_tensor(f"in_{name}_dram", a.shape, _mybir.dt.from_np(a.dtype), kind="ExternalInput").ap())
    for i, (shape, dtype) in enumerate(_OUTS):
        dt = _mybir.dt.from_np(_np.dtype(dtype))
        args.append(nc.dram_tensor(f"out_{i}_dram", shape, dt, kind="ExternalOutput").ap())
    gnn_two_layers(nc, *args)
    got = _run(nc, [arrays], core_ids=[0])
    return got.results[0]["out_0_dram"]
```

```python
from contextlib import ExitStack

import concourse.bass as bass
from concourse import mybir

P = 128
EPS = 1e-5
RING = 3

ALU = mybir.AluOpType
ACT = mybir.ActivationFunctionType
F32 = mybir.dt.float32
F32R = mybir.dt.float32r


def gnn_two_layers(nc, x, adj, w, bias, wq, wk, wv, out):
    B, N, D = x.shape
    T = N // P
    C = D // P
    assert T == 2 and C == 2 and N == D
    LOOP_FIRST = 3 * RING
    LOOP_END = (B - 2) // RING * RING

    class Batch:

        def __init__(self, turn, k, lag=0):
            self.b = RING * turn + (k - lag)
            self.slot = (k - lag) % RING
            self.uses = turn + (k - lag) // RING
            self.fixed = isinstance(turn, int)
            self.bank_reused = not self.fixed or self.b >= 1
            self.slot_reused = not self.fixed or self.b >= RING
            self.first = self.fixed and self.b == 0
            self.last = self.fixed and self.b == B - 1

    def batch(b):
        return Batch(b // RING, b % RING)

    with ExitStack() as ctx:
        def sb(name, shape, dt=F32):
            return ctx.enter_context(nc.sbuf_tensor(name, shape, dt))

        def bank(name):
            return ctx.enter_context(nc.psum_tensor(name, [P, 2, 256], F32))

        def sem(name):
            return ctx.enter_context(nc.semaphore(name))

        def ring(name, shape, dt=F32):
            return [sb(f"{name}{i}", shape, dt) for i in range(RING)]

        ident = sb("ident", [P, P])
        eps, root_of_eps = sb("eps", [P, 1]), sb("root_of_eps", [P, 1])
        adj_in = sb("adj_in", [P, T, N])
        w_in = sb("w_in", [P, C, D])
        wq_in = sb("wq_in", [P, C, D])
        wk_in = sb("wk_in", [P, C, D])
        wv_in = sb("wv_in", [P, C, D])
        bias_in = sb("bias_in", [P, T, D])
        ones = sb("ones", [P, P], F32R)
        adj_w = sb("adj_w", [P, T, N])
        adjT_h, adjT_l = sb("adjT_h", [P, T, N], F32R), sb("adjT_l", [P, T, N], F32R)
        w_h, w_l = sb("w_h", [P, C, D], F32R), sb("w_l", [P, C, D], F32R)
        wq_h, wq_l = sb("wq_h", [P, C, D], F32R), sb("wq_l", [P, C, D], F32R)
        wk_h, wk_l = sb("wk_h", [P, C, D], F32R), sb("wk_l", [P, C, D], F32R)
        a_h, a_l = sb("a_h", [P, C, D], F32R), sb("a_l", [P, C, D], F32R)
        wvT_h, wvT_l = sb("wvT_h", [P, C, D], F32R), sb("wvT_l", [P, C, D], F32R)

        x_in = ring("x_in", [P, T, D])
        x_h, x_l = ring("x_h", [P, T, D], F32R), ring("x_l", [P, T, D], F32R)
        xb = ring("xb", [P, T, D])
        yT_h, yT_l = ring("yT_h", [P, C, N], F32R), ring("yT_l", [P, C, N], F32R)
        r = ring("r", [P, T, D])
        x1 = ring("x1", [P, T, D])
        x1T_h, x1T_l = ring("x1T_h", [P, C, N], F32R), ring("x1T_l", [P, C, N], F32R)
        gT_h, gT_l = ring("gT_h", [P, C, N], F32R), ring("gT_l", [P, C, N], F32R)
        v_h, v_l = ring("v_h", [P, T, D], F32R), ring("v_l", [P, T, D], F32R)
        s = ring("s", [P, T, N])
        s_h, s_l = ring("s_h", [P, T, N], F32R), ring("s_l", [P, T, N], F32R)
        s_sq = ring("s_sq", [P, T, N])
        fold = ring("fold", [P, N])
        fold_h, fold_l = ring("fold_h", [P, N], F32R), ring("fold_l", [P, N], F32R)
        ssq_diag = ring("ssq_diag", [P, T, P])
        r2 = ring("r2", [P, T, D])
        x2 = ring("x2", [P, T, D])
        st1, st2 = ring("st1", [P, T, 6]), ring("st2", [P, T, 6])
        mv1, mv2 = ring("mv1", [P, T, 2]), ring("mv2", [P, T, 2])
        std1, std2 = ring("std1", [P, T]), ring("std2", [P, T])
        rstd1, rstd2 = ring("rstd1", [P, T]), ring("rstd2", [P, T])
        shift1, shift2 = ring("shift1", [P, T]), ring("shift2", [P, T])
        ssq, norm, inv_norm = ring("ssq", [P, T]), ring("norm", [P, T]), ring("inv_norm", [P, T])

        ps_y, ps_h, ps_x1T, ps_g = bank("ps_y"), bank("ps_h"), bank("ps_x1T"), bank("ps_g")
        ps_v, ps_rel, ps_ssq, ps_o = bank("ps_v"), bank("ps_rel"), bank("ps_ssq"), bank("ps_o")

        def o_bank(b):
            return ps_h if b.last else ps_o

        adj_loaded, w_loaded, bias_loaded = sem("adj_loaded"), sem("w_loaded"), sem("bias_loaded")
        wqk_loaded, wv_loaded = sem("wqk_loaded"), sem("wv_loaded")
        x_loaded = [sem(f"x_loaded{i}") for i in range(RING)]
        stored = [sem(f"stored{i}") for i in range(RING)]
        last_stored = sem("last_stored")
        ident_zeroed, ident_ready, eps_ready = sem("ident_zeroed"), sem("ident_ready"), sem("eps_ready")
        adjT_done, adj_w_ready, ones_ready = sem("adjT_done"), sem("adj_w_ready"), sem("ones_ready")
        adjT_h_ready, adjT_l_ready = sem("adjT_h_ready"), sem("adjT_l_ready")
        w_h_ready, w_l_ready = sem("w_h_ready"), sem("w_l_ready")
        wqk_h_ready, wqk_l_ready = sem("wqk_h_ready"), sem("wqk_l_ready")
        a_done, a_h_ready, a_l_ready = sem("a_done"), sem("a_h_ready"), sem("a_l_ready")
        wvT_done, wvT_h_ready, wvT_l_ready = sem("wvT_done"), sem("wvT_h_ready"), sem("wvT_l_ready")
        y_done, h_done, x1T_done, g_done = sem("y_done"), sem("h_done"), sem("x1T_done"), sem("g_done")
        v_done, rel_done, sum_done, o_done = sem("v_done"), sem("rel_done"), sem("sum_done"), sem("o_done")
        x_h_ready, x_l_ready = sem("x_h_ready"), sem("x_l_ready")
        yT_h_ready, yT_l_ready = sem("yT_h_ready"), sem("yT_l_ready")
        x1T_h_ready, x1T_l_ready = sem("x1T_h_ready"), sem("x1T_l_ready")
        gT_h_ready, gT_l_ready = sem("gT_h_ready"), sem("gT_l_ready")
        v_h_ready, v_l_ready = sem("v_h_ready"), sem("v_l_ready")
        s_h_ready, s_l_ready = sem("s_h_ready"), sem("s_l_ready")
        fold_h_ready, fold_l_ready = sem("fold_h_ready"), sem("fold_l_ready")
        last_s_l_ready, last_fold_ready, last_fold_l_ready = sem("last_s_l_ready"), sem("last_fold_ready"), sem("last_fold_l_ready")
        xb_ready, r_ready, s_ready = sem("xb_ready"), sem("r_ready"), sem("s_ready")
        sq_ready, fold_ready, ssq_halves = sem("sq_ready"), sem("fold_ready"), sem("ssq_halves")
        norm_ready, inv_norm_ready = sem("norm_ready"), sem("inv_norm_ready")
        r2_halves, x1_ready, x2_halves = sem("r2_halves"), sem("x1_ready"), sem("x2_halves")
        last_x2_0_ready, last_x2_1_ready = sem("last_x2_0_ready"), sem("last_x2_1_ready")
        st1_halves, st2_halves, mv1_ready, mv2_ready = sem("st1_halves"), sem("st2_halves"), sem("mv1_ready"), sem("mv2_ready")
        std1_ready, std2_ready, rstd1_ready, rstd2_ready = sem("std1_ready"), sem("std2_ready"), sem("rstd1_ready"), sem("rstd2_ready")
        shift1_ready, shift2_ready = sem("shift1_ready"), sem("shift2_ready")

        x_v = x.rearrange("b (p t) d -> b p t d", t=T)
        out_v = out.rearrange("b (p t) d -> b p t d", t=T)

        block = ctx.enter_context(nc.Block())

        @block.sync
        def _(sp):
            def load_x(b):
                if b.slot_reused:
                    sp.wait_ge(x_h_ready, b.b - RING + 1)
                    sp.wait_ge(x_l_ready, b.b - RING + 1)
                    sp.wait_ge(xb_ready, b.b - RING + 1)
                sp.dma_start(x_in[b.slot][:], x_v[b.b]).then_inc(x_loaded[b.slot], 16)

            def store(b):
                sp.wait_ge(x2_halves, 2 * b.b + 2)
                sp.dma_start(out_v[b.b], x2[b.slot][:]).then_inc(stored[b.slot], 16)

            sp.dma_start(adj_in[:], adj.rearrange("(p t) m -> p t m", t=T)).then_inc(adj_loaded, 16)
            sp.dma_start(w_in[:], w.rearrange("(c p) o -> p c o", p=P)).then_inc(w_loaded, 16)
            load_x(batch(1))
            sp.dma_start(wv_in[:], wv.rearrange("(c p) d -> p c d", p=P)).then_inc(wv_loaded, 16)
            sp.dma_start(wq_in[:], wq.rearrange("(p c) d -> p c d", c=C)).then_inc(wqk_loaded, 16)
            sp.dma_start(wk_in[:], wk.rearrange("(p c) d -> p c d", c=C)).then_inc(wqk_loaded, 16)
            for i in range(2, 5):
                load_x(batch(i))
            for i in range(3, LOOP_FIRST):
                load_x(batch(i + 2))
                if i >= 4:
                    store(batch(i - 4))
            with sp.Fori(LOOP_FIRST // RING, LOOP_END // RING) as turn:
                for k in range(RING):
                    load_x(Batch(turn, k, -2))
                    store(Batch(turn, k, 4))
            for i in range(LOOP_END - 4, B - 1):
                if i + 6 < B:
                    load_x(batch(i + 6))
                store(batch(i))
            sp.wait_ge(last_x2_0_ready, 1)
            sp.dma_start(out_v[B - 1, :, 0], x2[(B - 1) % RING][:, 0]).then_inc(stored[(B - 1) % RING], 16)
            for slot in range(RING):
                sp.wait_ge(stored[slot], 16 * len(range(slot, B, RING)))

        @block.tensor
        def _(pe):
            def product_half(j, result, stat_h, stat_l, mov_h, mov_l, await_mov_lo=None, await_stat_lo=None):
                cut = slice(j * P, (j + 1) * P)
                for c in range(2):
                    nc.tensor.matmul(result[:, j], stat_h[:, c, cut], mov_h[:, c], start=(c == 0), stop=False)
                if await_mov_lo:
                    await_mov_lo()
                for c in range(2):
                    nc.tensor.matmul(result[:, j], stat_h[:, c, cut], mov_l[:, c], start=False, stop=False)
                if await_stat_lo:
                    await_stat_lo()
                for c in range(2):
                    last = nc.tensor.matmul(result[:, j], stat_l[:, c, cut], mov_h[:, c], start=False, stop=(c == 1))
                return last

            def product(*operands, await_mov_lo=None, await_stat_lo=None):
                product_half(0, *operands, await_mov_lo, await_stat_lo)
                return product_half(1, *operands)

            def transposed(result, value):
                for c in range(2):
                    for t in range(2):
                        last = nc.tensor.transpose(result[:, c, t * P:(t + 1) * P],
                                                   value[:, t, c * P:(c + 1) * P], ident[:])
                return last

            def y_product(b):
                if b.bank_reused:
                    pe.wait_ge(yT_l_ready, b.b)
                pe.wait_ge(x_h_ready, b.b + 1)
                if b.first:
                    pe.wait_ge(adjT_h_ready, 1)

                product(ps_y, x_h[b.slot], x_l[b.slot], adjT_h, adjT_l,
                        await_mov_lo=(lambda: pe.wait_ge(adjT_l_ready, 1)) if b.first else None,
                        await_stat_lo=lambda: pe.wait_ge(x_l_ready, b.b + 1)).then_inc(y_done, 1)

            def h_product(b):
                if b.first:
                    pe.wait_ge(w_l_ready, 1)
                if b.bank_reused:
                    pe.wait_ge(r_ready, b.b)
                pe.wait_ge(yT_h_ready, b.b + 1)
                product(ps_h, yT_h[b.slot], yT_l[b.slot], w_h, w_l,
                        await_stat_lo=lambda: pe.wait_ge(yT_l_ready, b.b + 1)).then_inc(h_done, 1)

            def x1_transpose(b):
                if b.bank_reused:
                    pe.wait_ge(x1T_l_ready, b.b)
                pe.wait_ge(x1_ready, b.b + 1)
                transposed(ps_x1T, x1[b.slot]).then_inc(x1T_done, 1)

            def g_product(b):
                if b.first:
                    pe.wait_ge(a_l_ready, 1)
                if b.bank_reused:
                    pe.wait_ge(gT_l_ready, b.b)
                pe.wait_ge(x1T_h_ready, b.b + 1)
                product(ps_g, a_h, a_l, x1T_h[b.slot], x1T_l[b.slot],
                        await_mov_lo=lambda: pe.wait_ge(x1T_l_ready, b.b + 1)).then_inc(g_done, 1)

            def v_product(b):
                if b.first:
                    pe.wait_ge(wvT_l_ready, 1)
                if b.bank_reused:
                    pe.wait_ge(v_l_ready, b.b)
                product(ps_v, x1T_h[b.slot], x1T_l[b.slot], wvT_h, wvT_l).then_inc(v_done, 1)

            def rel_product(b):
                if b.bank_reused:
                    pe.wait_ge(s_ready, b.b)
                pe.wait_ge(gT_h_ready, b.b + 1)
                product(ps_rel, x1T_h[b.slot], x1T_l[b.slot], gT_h[b.slot], gT_l[b.slot],
                        await_mov_lo=lambda: pe.wait_ge(gT_l_ready, b.b + 1)).then_inc(rel_done, 1)

            def sum_squares(b):
                if b.bank_reused:
                    pe.wait_ge(ssq_halves, 2 * b.b)
                if b.last:
                    pe.wait_ge(last_fold_l_ready, 1)
                else:
                    pe.wait_ge(fold_l_ready, b.b + 1)
                nc.tensor.matmul(ps_ssq[:, 0], ones[:], fold_h[b.slot][:], start=True, stop=False)
                nc.tensor.matmul(ps_ssq[:, 0], ones[:], fold_l[b.slot][:], start=False, stop=True).then_inc(sum_done, 1)

            def await_s_lo(b):
                if b.last:
                    pe.wait_ge(last_s_l_ready, 1)
                else:
                    pe.wait_ge(s_l_ready, b.b + 1)

            def o_product(b):
                if b.last:
                    pe.wait_ge(r_ready, B)
                elif b.bank_reused:
                    pe.wait_ge(r2_halves, 2 * b.b)
                pe.wait_ge(v_l_ready, b.b + 1)
                pe.wait_ge(s_h_ready, b.b + 1)
                product(o_bank(b), s_h[b.slot], s_l[b.slot], v_h[b.slot], v_l[b.slot],
                        await_stat_lo=lambda: await_s_lo(b)).then_inc(o_done, 1)

            def o_product_halves(b, between):
                operands = (ps_o, s_h[b.slot], s_l[b.slot], v_h[b.slot], v_l[b.slot])
                pe.wait_ge(r2_halves, 2 * b.b)
                pe.wait_ge(v_l_ready, b.b + 1)
                pe.wait_ge(s_h_ready, b.b + 1)
                product_half(0, *operands, await_stat_lo=lambda: await_s_lo(b))
                between()
                product_half(1, *operands).then_inc(o_done, 1)

            def step(b0, b1, b2, b3):
                y_product(b0)
                sum_squares(b3)
                x1_transpose(b1)
                rel_product(b2)
                h_product(b0)
                g_product(b1)
                v_product(b1)
                o_product(b2)

            pe.wait_ge(ones_ready, 1)
            pe.wait_ge(ident_ready, 1)
            pe.wait_ge(adj_loaded, 16)
            for u in range(T):
                for t in range(T):
                    last = nc.tensor.transpose(ps_ssq[:, u, t * P:(t + 1) * P], adj_in[:, t, u::T], ident[:])
            last.then_inc(adjT_done, 1)
            y_product(batch(0))
            pe.wait_ge(wv_loaded, 16)
            transposed(ps_v, wv_in).then_inc(wvT_done, 1)
            h_product(batch(0))
            y_product(batch(1))
            pe.wait_ge(wqk_l_ready, 2)
            product(ps_g, wq_h, wq_l, wk_h, wk_l).then_inc(a_done, 1)
            h_product(batch(1))
            x1_transpose(batch(0))
            y_product(batch(2))
            g_product(batch(0))
            v_product(batch(0))
            x1_transpose(batch(1))
            rel_product(batch(0))
            h_product(batch(2))
            g_product(batch(1))
            v_product(batch(1))
            o_product(batch(0))
            for i in range(3, LOOP_FIRST):
                step(*(batch(i - lag) for lag in range(4)))
            with pe.Fori(LOOP_FIRST // RING, LOOP_END // RING) as turn:
                for k in range(RING):
                    step(*(Batch(turn, k, lag) for lag in range(4)))
            for i in range(LOOP_END, B - 1):
                step(*(batch(i - lag) for lag in range(4)))
            y_product(batch(B - 1))
            sum_squares(batch(B - 4))
            x1_transpose(batch(B - 2))
            rel_product(batch(B - 3))
            h_product(batch(B - 1))
            g_product(batch(B - 2))
            v_product(batch(B - 2))

            def while_layernorm_and_split_run():
                rel_product(batch(B - 2))
                sum_squares(batch(B - 3))
                x1_transpose(batch(B - 1))
            o_product_halves(batch(B - 3), while_layernorm_and_split_run)
            g_product(batch(B - 1))
            v_product(batch(B - 1))
            rel_product(batch(B - 1))
            o_product(batch(B - 2))
            sum_squares(batch(B - 2))
            o_product(batch(B - 1))
            sum_squares(batch(B - 1))

        @block.scalar
        def _(act):
            def x_hi(b):
                act.wait_ge(x_loaded[b.slot], 16 * b.uses + 16)
                if b.slot_reused:
                    act.wait_ge(y_done, b.b - RING + 1)
                nc.scalar.copy(x_h[b.slot][:], x_in[b.slot][:]).then_inc(x_h_ready, 1)

            def y_hi(b):
                act.wait_ge(y_done, b.b + 1)
                if b.slot_reused:
                    act.wait_ge(h_done, b.b - RING + 1)
                nc.scalar.copy(yT_h[b.slot][:], ps_y[:]).then_inc(yT_h_ready, 1)

            def std_1(b):
                act.wait_ge(mv1_ready, 2 * b.b + 2)
                nc.scalar.activation(std1[b.slot][:], mv1[b.slot][:, :, 1], ACT.Sqrt,
                                     bias=eps[:, 0:1]).then_inc(std1_ready, 1)

            def layernorm_1(b):
                act.wait_ge(shift1_ready, b.b + 1)
                if b.slot_reused:
                    act.wait_ge(r2_halves, 2 * (b.b - RING) + 2)
                for t in range(T):
                    last = nc.scalar.activation(x1[b.slot][:, t], r[b.slot][:, t], ACT.Identity,
                                                bias=shift1[b.slot][:, t:t + 1],
                                                scale=rstd1[b.slot][:, t:t + 1])
                last.then_inc(x1_ready, 1)

            def x1T_hi(b):
                act.wait_ge(x1T_done, b.b + 1)
                if b.slot_reused:
                    act.wait_ge(rel_done, b.b - RING + 1)
                nc.scalar.copy(x1T_h[b.slot][:], ps_x1T[:]).then_inc(x1T_h_ready, 1)

            def g_hi(b):
                act.wait_ge(g_done, b.b + 1)
                if b.slot_reused:
                    act.wait_ge(rel_done, b.b - RING + 1)
                nc.scalar.copy(gT_h[b.slot][:], ps_g[:]).then_inc(gT_h_ready, 1)

            def v_hi(b):
                act.wait_ge(v_done, b.b + 1)
                if b.slot_reused:
                    act.wait_ge(o_done, b.b - RING + 1)
                nc.scalar.copy(v_h[b.slot][:], ps_v[:]).then_inc(v_h_ready, 1)

            def s_hi(b):
                act.wait_ge(s_ready, b.b + 1)
                if b.slot_reused:
                    act.wait_ge(o_done, b.b - RING + 1)
                nc.scalar.copy(s_h[b.slot][:], s[b.slot][:]).then_inc(s_h_ready, 1)

            def square(b):
                nc.scalar.activation(s_sq[b.slot][:], s[b.slot][:], ACT.Square).then_inc(sq_ready, 1)

            def fold_hi(b):
                if b.last:
                    act.wait_ge(last_fold_ready, 1)
                else:
                    act.wait_ge(fold_ready, b.b + 1)
                if b.slot_reused:
                    act.wait_ge(sum_done, b.b - RING + 1)
                nc.scalar.copy(fold_h[b.slot][:], fold[b.slot][:]).then_inc(fold_h_ready, 1)

            def row_norm(b):
                act.wait_ge(ssq_halves, 2 * b.b + 2)
                nc.scalar.activation(norm[b.slot][:], ssq[b.slot][:], ACT.Sqrt).then_inc(norm_ready, 1)

            def std_2(b):
                act.wait_ge(mv2_ready, 2 * b.b + 2)
                nc.scalar.activation(std2[b.slot][:], mv2[b.slot][:, :, 1], ACT.Sqrt,
                                     bias=eps[:, 0:1]).then_inc(std2_ready, 1)

            def step(b_next, b0, b1, b2, b3, b4):
                y_hi(b0)
                x1T_hi(b1)
                row_norm(b3)
                if b4:
                    std_2(b4)
                if b_next:
                    x_hi(b_next)
                s_hi(b2)
                square(b2)
                g_hi(b1)
                fold_hi(b2)
                std_1(b0)
                v_hi(b1)
                layernorm_1(b0)

            act.dma_start(x_in[0][:], x_v[0]).then_inc(x_loaded[0], 16)
            act.wait_ge(eps_ready, 1)
            nc.scalar.activation(root_of_eps[:], eps[:], ACT.Sqrt)
            x_hi(batch(0))
            act.wait_ge(adjT_done, 1)
            nc.scalar.copy(adjT_h[:], ps_ssq[:]).then_inc(adjT_h_ready, 1)
            act.wait_ge(w_loaded, 16)
            nc.scalar.copy(w_h[:], w_in[:]).then_inc(w_h_ready, 1)
            y_hi(batch(0))
            x_hi(batch(1))
            act.wait_ge(wqk_loaded, 32)
            nc.scalar.copy(wq_h[:], wq_in[:]).then_inc(wqk_h_ready, 1)
            nc.scalar.copy(wk_h[:], wk_in[:]).then_inc(wqk_h_ready, 1)
            act.wait_ge(wvT_done, 1)
            nc.scalar.copy(wvT_h[:], ps_v[:]).then_inc(wvT_h_ready, 1)
            x_hi(batch(2))
            y_hi(batch(1))
            std_1(batch(0))
            act.wait_ge(a_done, 1)
            nc.scalar.copy(a_h[:], ps_g[:]).then_inc(a_h_ready, 1)
            layernorm_1(batch(0))
            x1T_hi(batch(0))
            std_1(batch(1))
            y_hi(batch(2))
            layernorm_1(batch(1))
            g_hi(batch(0))
            v_hi(batch(0))
            x1T_hi(batch(1))
            x_hi(batch(3))
            s_hi(batch(0))
            square(batch(0))
            g_hi(batch(1))
            fold_hi(batch(0))
            std_1(batch(2))
            v_hi(batch(1))
            layernorm_1(batch(2))
            for i in range(3, LOOP_FIRST):
                step(*(batch(i - lag) if i >= lag else None for lag in range(-1, 5)))
            with act.Fori(LOOP_FIRST // RING, LOOP_END // RING) as turn:
                for k in range(RING):
                    step(*(Batch(turn, k, lag) for lag in range(-1, 5)))
            for i in range(LOOP_END, B):
                step(*(batch(i - lag) if i - lag < B else None for lag in range(-1, 5)))
            x1T_hi(batch(B - 1))
            row_norm(batch(B - 3))
            s_hi(batch(B - 2))
            square(batch(B - 2))
            g_hi(batch(B - 1))
            fold_hi(batch(B - 2))
            v_hi(batch(B - 1))
            std_2(batch(B - 4))
            s_hi(batch(B - 1))
            square(batch(B - 1))
            fold_hi(batch(B - 1))
            std_2(batch(B - 3))
            row_norm(batch(B - 2))
            row_norm(batch(B - 1))
            std_2(batch(B - 2))
            std_2(batch(B - 1))
            last = batch(B - 1)
            act.wait_ge(stored[last.slot], 16 * last.uses)
            act.wait_ge(shift2_ready, B)
            nc.scalar.activation(x2[last.slot][:, 1], r2[last.slot][:, 1], ACT.Identity,
                                 bias=shift2[last.slot][:, 1:2], scale=rstd2[last.slot][:, 1:2]).then_inc(last_x2_1_ready, 1)
            act.wait_ge(last_x2_1_ready, 1)
            act.dma_start(out_v[B - 1, :, 1], x2[last.slot][:, 1]).then_inc(last_stored, 16)
            act.wait_ge(last_stored, 16)

        @block.vector
        def _(dve):
            def lo_part(dst, value, hi):
                return nc.vector.tensor_tensor(dst[:], value[:], hi[:].bitcast(F32), ALU.subtract)

            def y_lo(b):
                dve.wait_ge(yT_h_ready, b.b + 1)
                if b.slot_reused:
                    dve.wait_ge(h_done, b.b - RING + 1)
                lo_part(yT_l[b.slot], ps_y, yT_h[b.slot]).then_inc(yT_l_ready, 1)

            def residual_1(b):
                dve.wait_ge(h_done, b.b + 1)
                dve.wait_ge(xb_ready, b.b + 1)
                if b.slot_reused:
                    dve.wait_ge(x1_ready, b.b - RING + 1)
                nc.vector.tensor_tensor(r[b.slot][:], ps_h[:], xb[b.slot][:], ALU.add).then_inc(r_ready, 1)

            def statistics_1(b):
                dve.wait_ge(r_ready, b.b + 1)
                for t in range(T):
                    nc.vector.bn_stats(st1[b.slot][:, t], r[b.slot][:, t]).then_inc(st1_halves, 1)

            def variance_1(b):
                for t in range(T):
                    nc.vector.bn_aggr(mv1[b.slot][:, t], st1[b.slot][:, t]).then_inc(mv1_ready, 1)

            def scale_and_shift_1(b):
                dve.wait_ge(std1_ready, b.b + 1)
                nc.vector.reciprocal(rstd1[b.slot][:], std1[b.slot][:]).then_inc(rstd1_ready, 1)
                dve.wait_ge(rstd1_ready, b.b + 1)
                nc.vector.scalar_tensor_tensor(shift1[b.slot][:], mv1[b.slot][:, :, 0], -1.0, rstd1[b.slot][:],
                                               ALU.mult, ALU.mult).then_inc(shift1_ready, 1)

            def x1T_lo(b):
                dve.wait_ge(x1T_h_ready, b.b + 1)
                if b.slot_reused:
                    dve.wait_ge(rel_done, b.b - RING + 1)
                lo_part(x1T_l[b.slot], ps_x1T, x1T_h[b.slot]).then_inc(x1T_l_ready, 1)

            def g_lo(b):
                dve.wait_ge(gT_h_ready, b.b + 1)
                if b.slot_reused:
                    dve.wait_ge(rel_done, b.b - RING + 1)
                lo_part(gT_l[b.slot], ps_g, gT_h[b.slot]).then_inc(gT_l_ready, 1)

            def v_lo(b):
                dve.wait_ge(v_h_ready, b.b + 1)
                if b.slot_reused:
                    dve.wait_ge(o_done, b.b - RING + 1)
                lo_part(v_l[b.slot], ps_v, v_h[b.slot]).then_inc(v_l_ready, 1)

            def weigh(b):
                dve.wait_ge(rel_done, b.b + 1)
                if b.slot_reused:
                    dve.wait_ge(sq_ready, b.b - RING + 1)
                    dve.wait_ge(s_l_ready, b.b - RING + 1)
                nc.vector.tensor_tensor(s[b.slot][:], ps_rel[:], adj_w[:], ALU.mult).then_inc(s_ready, 1)

            def pick_sums(b):
                dve.wait_ge(sum_done, b.b + 1)
                for t in range(T):
                    nc.vector.tensor_tensor_reduce(out=ssq_diag[b.slot][:, t], in0=ps_ssq[:, 0, t * P:(t + 1) * P],
                                                   in1=ident[:], scale=1.0, scalar=0.0, op0=ALU.mult, op1=ALU.add,
                                                   accum_out=ssq[b.slot][:, t:t + 1]).then_inc(ssq_halves, 1)

            def invert_norm(b):
                dve.wait_ge(norm_ready, b.b + 1)
                nc.vector.reciprocal(inv_norm[b.slot][:], norm[b.slot][:]).then_inc(inv_norm_ready, 1)

            def residual_2(b):
                dve.wait_ge(o_done, b.b + 1)
                dve.wait_ge(inv_norm_ready, b.b + 1)
                if b.slot_reused:
                    dve.wait_ge(x2_halves, 2 * (b.b - RING) + 2)
                for t in range(T):
                    nc.vector.scalar_tensor_tensor(r2[b.slot][:, t], o_bank(b)[:, t], inv_norm[b.slot][:, t:t + 1],
                                                   x1[b.slot][:, t], ALU.mult, ALU.add).then_inc(r2_halves, 1)

            def statistics_2_half(b, t):
                dve.wait_ge(r2_halves, 2 * b.b + 1 + t)
                nc.vector.bn_stats(st2[b.slot][:, t], r2[b.slot][:, t]).then_inc(st2_halves, 1)

            def statistics_2(b):
                for t in range(T):
                    statistics_2_half(b, t)

            def variance_2(b):
                for t in range(T):
                    nc.vector.bn_aggr(mv2[b.slot][:, t], st2[b.slot][:, t]).then_inc(mv2_ready, 1)

            def scale_2(b):
                dve.wait_ge(std2_ready, b.b + 1)
                nc.vector.reciprocal(rstd2[b.slot][:], std2[b.slot][:]).then_inc(rstd2_ready, 1)

            def shift_2(b):
                dve.wait_ge(rstd2_ready, b.b + 1)
                nc.vector.scalar_tensor_tensor(shift2[b.slot][:], mv2[b.slot][:, :, 0], -1.0, rstd2[b.slot][:],
                                               ALU.mult, ALU.mult).then_inc(shift2_ready, 1)

            def step(b0, b1, b2, b3, b4):
                if b4:
                    statistics_2(b4)
                    dve.wait_ge(st2_halves, 2 * b4.b + 2)
                pick_sums(b3)
                if b4:
                    variance_2(b4)
                y_lo(b0)
                x1T_lo(b1)
                invert_norm(b3)
                weigh(b2)
                residual_2(b3)
                v_lo(b2)
                residual_1(b0)
                statistics_1(b0)
                dve.wait_ge(st1_halves, 2 * b0.b + 2)
                if b4:
                    scale_2(b4)
                variance_1(b0)
                g_lo(b1)
                if b4:
                    shift_2(b4)
                scale_and_shift_1(b0)

            nc.vector.memset(eps[:], EPS).then_inc(eps_ready, 1)
            nc.vector.memset(ones[:].bitcast(F32), 1.0).then_inc(ones_ready, 1)
            dve.wait_ge(adjT_h_ready, 1)
            lo_part(adjT_l, ps_ssq, adjT_h).then_inc(adjT_l_ready, 1)
            nc.vector.tensor_copy(adj_w[:].rearrange("p u (t q) -> p u t q", t=T),
                                  adj_in[:].rearrange("p u (q t) -> p u t q", t=T)).then_inc(adj_w_ready, 1)
            dve.wait_ge(w_h_ready, 1)
            lo_part(w_l, w_in, w_h).then_inc(w_l_ready, 1)
            y_lo(batch(0))
            dve.wait_ge(wqk_h_ready, 1)
            lo_part(wq_l, wq_in, wq_h).then_inc(wqk_l_ready, 1)
            dve.wait_ge(wqk_h_ready, 2)
            lo_part(wk_l, wk_in, wk_h).then_inc(wqk_l_ready, 1)
            residual_1(batch(0))
            statistics_1(batch(0))
            dve.wait_ge(st1_halves, 2)
            variance_1(batch(0))
            y_lo(batch(1))
            scale_and_shift_1(batch(0))
            dve.wait_ge(wvT_h_ready, 1)
            lo_part(wvT_l, ps_v, wvT_h).then_inc(wvT_l_ready, 1)
            dve.wait_ge(a_h_ready, 1)
            lo_part(a_l, ps_g, a_h).then_inc(a_l_ready, 1)
            residual_1(batch(1))
            statistics_1(batch(1))
            x1T_lo(batch(0))
            dve.wait_ge(st1_halves, 4)
            variance_1(batch(1))
            scale_and_shift_1(batch(1))
            y_lo(batch(2))
            g_lo(batch(0))
            v_lo(batch(0))
            x1T_lo(batch(1))
            dve.wait_ge(adj_w_ready, 1)
            weigh(batch(0))
            residual_1(batch(2))
            statistics_1(batch(2))
            dve.wait_ge(st1_halves, 6)
            variance_1(batch(2))
            g_lo(batch(1))
            scale_and_shift_1(batch(2))
            for i in range(3, LOOP_FIRST):
                step(*(batch(i - lag) if i >= lag else None for lag in range(5)))
            with dve.Fori(LOOP_FIRST // RING, LOOP_END // RING) as turn:
                for k in range(RING):
                    step(*(Batch(turn, k, lag) for lag in range(5)))
            for i in range(LOOP_END, B):
                step(*(batch(i - lag) for lag in range(5)))
            weigh(batch(B - 2))
            pick_sums(batch(B - 3))
            x1T_lo(batch(B - 1))
            invert_norm(batch(B - 3))
            v_lo(batch(B - 2))
            residual_2(batch(B - 3))
            statistics_2(batch(B - 4))
            g_lo(batch(B - 1))
            dve.wait_ge(st2_halves, 2 * (B - 4) + 2)
            statistics_2_half(batch(B - 3), 0)
            variance_2(batch(B - 4))
            statistics_2_half(batch(B - 3), 1)
            v_lo(batch(B - 1))
            weigh(batch(B - 1))
            scale_2(batch(B - 4))
            shift_2(batch(B - 4))
            dve.wait_ge(st2_halves, 2 * (B - 3) + 2)
            variance_2(batch(B - 3))
            last = batch(B - 1)
            dve.wait_ge(s_h_ready, B)
            dve.wait_ge(o_done, B - RING)
            lo_part(s_l[last.slot], s[last.slot], s_h[last.slot]).then_inc(last_s_l_ready, 1)
            dve.wait_ge(sq_ready, B)
            dve.wait_ge(fold_l_ready, B - RING)
            nc.vector.tensor_tensor(fold[last.slot][:], s_sq[last.slot][:, 0], s_sq[last.slot][:, 1],
                                    ALU.add).then_inc(last_fold_ready, 1)
            pick_sums(batch(B - 2))
            dve.wait_ge(fold_h_ready, B)
            dve.wait_ge(sum_done, B - RING)
            lo_part(fold_l[last.slot], fold[last.slot], fold_h[last.slot]).then_inc(last_fold_l_ready, 1)
            invert_norm(batch(B - 2))
            scale_2(batch(B - 3))
            residual_2(batch(B - 2))
            pick_sums(batch(B - 1))
            shift_2(batch(B - 3))
            statistics_2_half(batch(B - 2), 0)
            invert_norm(batch(B - 1))
            statistics_2_half(batch(B - 2), 1)
            residual_2(batch(B - 1))
            dve.wait_ge(st2_halves, 2 * (B - 2) + 2)
            statistics_2_half(batch(B - 1), 0)
            variance_2(batch(B - 2))
            statistics_2_half(batch(B - 1), 1)
            dve.wait_ge(st2_halves, 2 * (B - 1) + 2)
            scale_2(batch(B - 2))
            variance_2(batch(B - 1))
            shift_2(batch(B - 2))
            scale_2(batch(B - 1))
            shift_2(batch(B - 1))
            dve.wait_ge(stored[last.slot], 16 * last.uses)
            nc.vector.tensor_scalar(x2[last.slot][:, 0], r2[last.slot][:, 0], mv2[last.slot][:, 0, 0:1],
                                    rstd2[last.slot][:, 0:1], ALU.subtract, ALU.mult).then_inc(last_x2_0_ready, 1)

        @block.gpsimd
        def _(pool):
            def x_lo(b):
                pool.wait_ge(x_h_ready, b.b + 1)
                if b.slot_reused:
                    pool.wait_ge(y_done, b.b - RING + 1)
                nc.gpsimd.tensor_tensor(x_l[b.slot][:], x_in[b.slot][:], x_h[b.slot][:].bitcast(F32),
                                        ALU.subtract).then_inc(x_l_ready, 1)

            def add_bias(b):
                if b.slot_reused:
                    pool.wait_ge(r_ready, b.b - RING + 1)
                nc.gpsimd.tensor_tensor(xb[b.slot][:], x_in[b.slot][:], bias_in[:], ALU.add).then_inc(xb_ready, 1)

            def await_layernorm_2(b):
                pool.wait_ge(shift2_ready, b.b + 1)
                if b.slot_reused:
                    pool.wait_ge(stored[b.slot], 16 * b.uses)

            def layernorm_2(b):
                for t in range(T):
                    nc.gpsimd.tensor_scalar(x2[b.slot][:, t], r2[b.slot][:, t], rstd2[b.slot][:, t:t + 1],
                                            shift2[b.slot][:, t:t + 1], ALU.mult, ALU.add).then_inc(x2_halves, 1)

            def s_lo(b):
                pool.wait_ge(s_h_ready, b.b + 1)
                if b.slot_reused:
                    pool.wait_ge(o_done, b.b - RING + 1)
                nc.gpsimd.tensor_tensor(s_l[b.slot][:], s[b.slot][:], s_h[b.slot][:].bitcast(F32),
                                        ALU.subtract).then_inc(s_l_ready, 1)

            def fold_squares(b):
                pool.wait_ge(sq_ready, b.b + 1)
                if b.slot_reused:
                    pool.wait_ge(fold_l_ready, b.b - RING + 1)
                nc.gpsimd.tensor_tensor(fold[b.slot][:], s_sq[b.slot][:, 0], s_sq[b.slot][:, 1],
                                        ALU.add).then_inc(fold_ready, 1)

            def fold_lo(b):
                pool.wait_ge(fold_h_ready, b.b + 1)
                if b.slot_reused:
                    pool.wait_ge(sum_done, b.b - RING + 1)
                nc.gpsimd.tensor_tensor(fold_l[b.slot][:], fold[b.slot][:], fold_h[b.slot][:].bitcast(F32),
                                        ALU.subtract).then_inc(fold_l_ready, 1)

            def step(b_next, b2, b4):
                if b_next:
                    x_lo(b_next)
                s_lo(b2)
                fold_squares(b2)
                fold_lo(b2)
                if b4:
                    await_layernorm_2(b4)
                if b_next:
                    add_bias(b_next)
                if b4:
                    layernorm_2(b4)

            nc.gpsimd.memset(ident[:], 0.0).then_inc(ident_zeroed, 1)
            pool.wait_ge(ident_zeroed, 1)
            nc.gpsimd.affine_select(out=ident[:], in_=ident[:], compare_op=ALU.not_equal, fill=1.0, base=0,
                                    pattern=[[-1, P]], channel_multiplier=1).then_inc(ident_ready, 1)
            pool.dma_start(bias_in[:], bias.partition_broadcast(P).rearrange("p (a d) -> p a d", a=1)
                           .to_broadcast([P, T, D])).then_inc(bias_loaded, 16)
            x_lo(batch(0))
            pool.wait_ge(bias_loaded, 16)
            add_bias(batch(0))
            for i in range(1, 3):
                x_lo(batch(i))
                add_bias(batch(i))
            step(batch(3), batch(0), None)
            for i in range(3, LOOP_FIRST):
                step(batch(i + 1), batch(i - 2), batch(i - 4) if i >= 4 else None)
            with pool.Fori(LOOP_FIRST // RING, LOOP_END // RING) as turn:
                for k in range(RING):
                    step(Batch(turn, k, -1), Batch(turn, k, 2), Batch(turn, k, 4))
            for i in range(LOOP_END, B):
                step(batch(i + 1) if i + 1 < B else None, batch(i - 2), batch(i - 4))
            s_lo(batch(B - 2))
            fold_squares(batch(B - 2))
            fold_lo(batch(B - 2))
            await_layernorm_2(batch(B - 4))
            layernorm_2(batch(B - 4))
            await_layernorm_2(batch(B - 3))
            layernorm_2(batch(B - 3))
            await_layernorm_2(batch(B - 2))
            layernorm_2(batch(B - 2))


_INS = ["x", "adj", "L0_gnn_weight", "L0_gnn_bias", "L1_gnn_Wq", "L1_gnn_Wk", "L1_gnn_Wv"]
_OUTS = [((32, 256, 256), "float32")]


def kernel(**inputs):
    import numpy as _np
    import concourse.bacc as _bacc
    from concourse import mybir as _mybir
    from concourse.bass_utils import run_bass_kernel_spmd as _run

    nc = _bacc.Bacc("TRN2", target_bir_lowering=False, num_devices=1)
    arrays, args = {}, []
    for name in _INS:
        a = _np.ascontiguousarray(inputs[name])
        arrays[f"in_{name}_dram"] = a
        args.append(nc.dram_tensor(f"in_{name}_dram", a.shape, _mybir.dt.from_np(a.dtype), kind="ExternalInput").ap())
    for i, (shape, dtype) in enumerate(_OUTS):
        dt = _mybir.dt.from_np(_np.dtype(dtype))
        args.append(nc.dram_tensor(f"out_{i}_dram", shape, dt, kind="ExternalOutput").ap())
    gnn_two_layers(nc, *args)
    got = _run(nc, [arrays], core_ids=[0])
    return got.results[0]["out_0_dram"]
```
